# Optimizing a Trainium2 kernel written in Bass

```python
import numpy as np
import jax
import jax.numpy as jnp

def _softmax(x, axis=-1):
    return jax.nn.softmax(x, axis=axis)

def _gelu(x):
    return jax.nn.gelu(x, approximate=True)

def _silu(x):
    return jax.nn.silu(x)

def _sigmoid(x):
    return jax.nn.sigmoid(x)

def _layernorm(x, axis=-1, eps=1e-05):
    m = jnp.mean(x, axis=axis, keepdims=True)
    v = jnp.var(x, axis=axis, keepdims=True)
    return (x - m) / jnp.sqrt(v + eps)

def _scatter_add(tgt, idx, src, axis=0):
    return tgt.at[idx].add(src)

def _segment_sum(src, seg, n):
    return jax.ops.segment_sum(src, seg, n)
kernel_name = 'mk_xattn_seq_d4_seqx_r8_248a11'

def setup_inputs(seed: int=0):
    np.random.seed(seed)
    _w = jnp.asarray

    def _rec_inputs():
        import jax
        import jax.numpy as jnp
        _rk = jax.random.key(seed)
        x = 7.22e-05 + 1 * jax.random.normal(jax.random.fold_in(_rk, 1), (8, 128, 128), jnp.float32)
        _lenS = 128 - jax.random.randint(jax.random.fold_in(_rk, 7), (8,), 0, max(1, 128 // 4) + 1, jnp.int32)
        _lenS2 = 128 - jax.random.randint(jax.random.fold_in(_rk, 8), (8,), 0, max(1, 128 // 4) + 1, jnp.int32)
        _ctx_2048P = jax.random.normal(jax.random.fold_in(_rk, 11), (8, 16, 256), jnp.float32)
        _ctx_2048c = jax.random.dirichlet(jax.random.fold_in(_rk, 511), 0.3 * jnp.ones((16,), jnp.float32), (8, 128))
        _ctx_2048t = jnp.einsum('bsk,bkd->bsd', _ctx_2048c, _ctx_2048P)
        _ctx_2048t = _ctx_2048t * jax.lax.rsqrt(jnp.mean(jnp.square(_ctx_2048t)) + 1e-12) * 0.953939
        ctx_2048 = -1.39393e-06 + 0.999914 * (_ctx_2048t + 0.3 * jax.random.normal(jax.random.fold_in(_rk, 611), (8, 128, 256), jnp.float32))
        _validS = jnp.arange(128)[None, :] < _lenS[:, None]
        _validS2 = jnp.arange(128)[None, :] < _lenS2[:, None]
        _causal = jnp.tril(jnp.ones((128, 128), dtype=bool))
        mask_S_fk1 = jnp.where(_validS[0], 1.0, 0.0).astype(jnp.float32)
        mask_S_fk0 = jnp.where(_validS[0], 0.0, 1.0).astype(jnp.float32)
        return (x, ctx_2048, mask_S_fk1, mask_S_fk0)
    x, ctx_2048, mask_S_fk1, mask_S_fk0 = _rec_inputs()

    def _L0_xattn_setup():
        import jax, jax.numpy as jnp
        import numpy as np
        D_MODEL = 128
        N_HEADS = 16
        N_KV_HEADS = 4
        HEAD_DIM = D_MODEL // N_HEADS
        SPEAKER_DIM = 256
        EPS = 1e-05

        def rmsnorm(x, w, eps=EPS):
            xf = x.astype(jnp.float32)
            inv = jax.lax.rsqrt(jnp.mean(xf * xf, axis=-1, keepdims=True) + eps)
            return (xf * inv).astype(x.dtype) * w
        key = jax.random.key(seed)
        ks = jax.random.split(key, 7)
        B, T, S = (4, 256, 64)
        x = jax.random.normal(ks[0], (B, T, D_MODEL), dtype=jnp.float32)
        cond = jax.random.normal(ks[1], (B, S, SPEAKER_DIM), dtype=jnp.float32)
        sq = 0.02
        wq = jax.random.normal(ks[2], (D_MODEL, N_HEADS * HEAD_DIM), dtype=jnp.float32) * sq
        wk = jax.random.normal(ks[3], (SPEAKER_DIM, N_KV_HEADS * HEAD_DIM), dtype=jnp.float32) * sq
        wv = jax.random.normal(ks[4], (SPEAKER_DIM, N_KV_HEADS * HEAD_DIM), dtype=jnp.float32) * sq
        wo = jax.random.normal(ks[5], (N_HEADS * HEAD_DIM, D_MODEL), dtype=jnp.float32) * sq
        norm_w = jnp.ones((D_MODEL,), dtype=jnp.float32)
        return {'x': x, 'cond': cond, 'wq': wq, 'wk': wk, 'wv': wv, 'wo': wo, 'norm_w': norm_w}
    _L0_xattn_all = _L0_xattn_setup()
    _L0_xattn_in = {k: v for k, v in _L0_xattn_all.items() if k in ('wq', 'wk', 'wv', 'wo', 'norm_w')}
    del _L0_xattn_all

    def _L1_xattn_setup():
        import jax, jax.numpy as jnp
        import numpy as np
        HEADS = 16
        HEAD_DIM = 64
        SUPPRESS = 20.0
        key = jax.random.key(seed)
        ks = jax.random.split(key, 8)
        B, HW, C, T, CT = (8, 512, 128, 77, 256)
        inner = HEADS * HEAD_DIM
        scale = 0.02
        return {'hidden_states': jax.random.normal(ks[0], (B, HW, C), jnp.float32), 'encoder_hidden_states': jax.random.normal(ks[1], (B, T, CT), jnp.float32), 'mask_A': (jax.random.uniform(ks[2], (HW,)) > 0.5).astype(jnp.float32), 'mask_B': (jax.random.uniform(ks[3], (HW,)) > 0.5).astype(jnp.float32), 'Wq': jax.random.normal(ks[4], (C, inner), jnp.float32) * scale, 'Wk': jax.random.normal(ks[5], (CT, inner), jnp.float32) * scale, 'Wv': jax.random.normal(ks[6], (CT, inner), jnp.float32) * scale, 'Wo': jax.random.normal(ks[7], (inner, C), jnp.float32) * scale, 'bo': jnp.zeros((C,), jnp.float32), 'token_indices_A': jnp.array([2, 3], dtype=jnp.int64), 'token_indices_B': jnp.array([5, 6], dtype=jnp.int64)}
    _L1_xattn_all = _L1_xattn_setup()
    _L1_xattn_in = {k: v for k, v in _L1_xattn_all.items() if k in ('Wq', 'Wk', 'Wv', 'Wo', 'bo', 'token_indices_A', 'token_indices_B')}
    del _L1_xattn_all

    def _L2_xattn_setup():
        import jax, jax.numpy as jnp
        import numpy as np
        HEADS = 16
        HEAD_DIM = 64
        SUPPRESS = 20.0
        key = jax.random.key(seed)
        ks = jax.random.split(key, 8)
        B, HW, C, T, CT = (8, 512, 128, 77, 256)
        inner = HEADS * HEAD_DIM
        scale = 0.02
        return {'hidden_states': jax.random.normal(ks[0], (B, HW, C), jnp.float32), 'encoder_hidden_states': jax.random.normal(ks[1], (B, T, CT), jnp.float32), 'mask_A': (jax.random.uniform(ks[2], (HW,)) > 0.5).astype(jnp.float32), 'mask_B': (jax.random.uniform(ks[3], (HW,)) > 0.5).astype(jnp.float32), 'Wq': jax.random.normal(ks[4], (C, inner), jnp.float32) * scale, 'Wk': jax.random.normal(ks[5], (CT, inner), jnp.float32) * scale, 'Wv': jax.random.normal(ks[6], (CT, inner), jnp.float32) * scale, 'Wo': jax.random.normal(ks[7], (inner, C), jnp.float32) * scale, 'bo': jnp.zeros((C,), jnp.float32), 'token_indices_A': jnp.array([2, 3], dtype=jnp.int64), 'token_indices_B': jnp.array([5, 6], dtype=jnp.int64)}
    _L2_xattn_all = _L2_xattn_setup()
    _L2_xattn_in = {k: v for k, v in _L2_xattn_all.items() if k in ('Wq', 'Wk', 'Wv', 'Wo', 'bo', 'token_indices_A', 'token_indices_B')}
    del _L2_xattn_all

    def _L3_xattn_setup():
        import jax, jax.numpy as jnp
        import numpy as np
        D_MODEL = 128
        N_HEADS = 16
        N_KV_HEADS = 4
        HEAD_DIM = D_MODEL // N_HEADS
        SPEAKER_DIM = 256
        EPS = 1e-05

        def rmsnorm(x, w, eps=EPS):
            xf = x.astype(jnp.float32)
            inv = jax.lax.rsqrt(jnp.mean(xf * xf, axis=-1, keepdims=True) + eps)
            return (xf * inv).astype(x.dtype) * w
        key = jax.random.key(seed)
        ks = jax.random.split(key, 7)
        B, T, S = (4, 256, 64)
        x = jax.random.normal(ks[0], (B, T, D_MODEL), dtype=jnp.float32)
        cond = jax.random.normal(ks[1], (B, S, SPEAKER_DIM), dtype=jnp.float32)
        sq = 0.02
        wq = jax.random.normal(ks[2], (D_MODEL, N_HEADS * HEAD_DIM), dtype=jnp.float32) * sq
        wk = jax.random.normal(ks[3], (SPEAKER_DIM, N_KV_HEADS * HEAD_DIM), dtype=jnp.float32) * sq
        wv = jax.random.normal(ks[4], (SPEAKER_DIM, N_KV_HEADS * HEAD_DIM), dtype=jnp.float32) * sq
        wo = jax.random.normal(ks[5], (N_HEADS * HEAD_DIM, D_MODEL), dtype=jnp.float32) * sq
        norm_w = jnp.ones((D_MODEL,), dtype=jnp.float32)
        return {'x': x, 'cond': cond, 'wq': wq, 'wk': wk, 'wv': wv, 'wo': wo, 'norm_w': norm_w}
    _L3_xattn_all = _L3_xattn_setup()
    _L3_xattn_in = {k: v for k, v in _L3_xattn_all.items() if k in ('wq', 'wk', 'wv', 'wo', 'norm_w')}
    del _L3_xattn_all
    return {'x': x, 'ctx_2048': ctx_2048, 'mask_S_fk1': mask_S_fk1, 'mask_S_fk0': mask_S_fk0, 'L0_xattn_wq': _L0_xattn_in['wq'], 'L0_xattn_wk': _L0_xattn_in['wk'], 'L0_xattn_wv': _L0_xattn_in['wv'], 'L0_xattn_wo': _L0_xattn_in['wo'], 'L0_xattn_norm_w': _L0_xattn_in['norm_w'], 'L1_xattn_Wq': _L1_xattn_in['Wq'], 'L1_xattn_Wk': _L1_xattn_in['Wk'], 'L1_xattn_Wv': _L1_xattn_in['Wv'], 'L1_xattn_Wo': _L1_xattn_in['Wo'], 'L1_xattn_bo': _L1_xattn_in['bo'], 'L1_xattn_token_indices_A': _L1_xattn_in['token_indices_A'], 'L1_xattn_token_indices_B': _L1_xattn_in['token_indices_B'], 'L2_xattn_Wq': _L2_xattn_in['Wq'], 'L2_xattn_Wk': _L2_xattn_in['Wk'], 'L2_xattn_Wv': _L2_xattn_in['Wv'], 'L2_xattn_Wo': _L2_xattn_in['Wo'], 'L2_xattn_bo': _L2_xattn_in['bo'], 'L2_xattn_token_indices_A': _L2_xattn_in['token_indices_A'], 'L2_xattn_token_indices_B': _L2_xattn_in['token_indices_B'], 'L3_xattn_wq': _L3_xattn_in['wq'], 'L3_xattn_wk': _L3_xattn_in['wk'], 'L3_xattn_wv': _L3_xattn_in['wv'], 'L3_xattn_wo': _L3_xattn_in['wo'], 'L3_xattn_norm_w': _L3_xattn_in['norm_w']}

def reference(x, ctx_2048, mask_S_fk1, mask_S_fk0, L0_xattn_wq, L0_xattn_wk, L0_xattn_wv, L0_xattn_wo, L0_xattn_norm_w, L1_xattn_Wq, L1_xattn_Wk, L1_xattn_Wv, L1_xattn_Wo, L1_xattn_bo, L1_xattn_token_indices_A, L1_xattn_token_indices_B, L2_xattn_Wq, L2_xattn_Wk, L2_xattn_Wv, L2_xattn_Wo, L2_xattn_bo, L2_xattn_token_indices_A, L2_xattn_token_indices_B, L3_xattn_wq, L3_xattn_wk, L3_xattn_wv, L3_xattn_wo, L3_xattn_norm_w):
    import jax
    import jax.numpy as jnp

    def _L0_xattn_ref(x, cond, wq, wk, wv, wo, norm_w):
        import jax, jax.numpy as jnp
        import numpy as np
        D_MODEL = 128
        N_HEADS = 16
        N_KV_HEADS = 4
        HEAD_DIM = D_MODEL // N_HEADS
        SPEAKER_DIM = 256
        EPS = 1e-05

        def rmsnorm(x, w, eps=EPS):
            xf = x.astype(jnp.float32)
            inv = jax.lax.rsqrt(jnp.mean(xf * xf, axis=-1, keepdims=True) + eps)
            return (xf * inv).astype(x.dtype) * w
        B, T, _ = x.shape
        S = cond.shape[1]
        n_rep = N_HEADS // N_KV_HEADS
        residual = x
        xn = rmsnorm(x, norm_w)
        q = (xn @ wq).reshape(B, T, N_HEADS, HEAD_DIM)
        k = (cond @ wk).reshape(B, S, N_KV_HEADS, HEAD_DIM)
        v = (cond @ wv).reshape(B, S, N_KV_HEADS, HEAD_DIM)
        qg = q.reshape(B, T, N_KV_HEADS, n_rep, HEAD_DIM)
        scale = 1.0 / np.sqrt(HEAD_DIM).astype(np.float32)
        scores = jnp.einsum('btgrd,bsgd->bgrts', qg, k) * scale
        attn = jax.nn.softmax(scores.astype(jnp.float32), axis=-1).astype(q.dtype)
        out = jnp.einsum('bgrts,bsgd->btgrd', attn, v).reshape(B, T, N_HEADS * HEAD_DIM)
        return residual + out @ wo

    def _L1_xattn_ref(hidden_states, encoder_hidden_states, mask_A, mask_B, Wq, Wk, Wv, Wo, bo, token_indices_A, token_indices_B):
        import jax, jax.numpy as jnp
        import numpy as np
        HEADS = 16
        HEAD_DIM = 64
        SUPPRESS = 20.0
        B, HW, C = hidden_states.shape
        T = encoder_hidden_states.shape[1]
        residual = hidden_states
        q = hidden_states @ Wq
        k = encoder_hidden_states @ Wk
        v = encoder_hidden_states @ Wv
        q = q.reshape(B, HW, HEADS, HEAD_DIM).transpose(0, 2, 1, 3)
        k = k.reshape(B, T, HEADS, HEAD_DIM).transpose(0, 2, 1, 3)
        v = v.reshape(B, T, HEADS, HEAD_DIM).transpose(0, 2, 1, 3)
        scale = HEAD_DIM ** (-0.5)
        logits = jnp.einsum('bhqd,bhkd->bhqk', q, k) * scale
        suppress_A_in = 1.0 - mask_A
        suppress_B_in = 1.0 - mask_B
        col_bias = jnp.zeros((HW, T), logits.dtype)
        col_bias = col_bias.at[:, token_indices_A].set((-SUPPRESS * suppress_A_in)[:, None])
        col_bias = col_bias.at[:, token_indices_B].set((-SUPPRESS * suppress_B_in)[:, None])
        logits = logits + col_bias[None, None, :, :]
        probs = jax.nn.softmax(logits, axis=-1)
        out = jnp.einsum('bhqk,bhkd->bhqd', probs, v)
        out = out.transpose(0, 2, 1, 3).reshape(B, HW, HEADS * HEAD_DIM)
        out = out @ Wo + bo
        out = out + residual
        return out

    def _L2_xattn_ref(hidden_states, encoder_hidden_states, mask_A, mask_B, Wq, Wk, Wv, Wo, bo, token_indices_A, token_indices_B):
        import jax, jax.numpy as jnp
        import numpy as np
        HEADS = 16
        HEAD_DIM = 64
        SUPPRESS = 20.0
        B, HW, C = hidden_states.shape
        T = encoder_hidden_states.shape[1]
        residual = hidden_states
        q = hidden_states @ Wq
        k = encoder_hidden_states @ Wk
        v = encoder_hidden_states @ Wv
        q = q.reshape(B, HW, HEADS, HEAD_DIM).transpose(0, 2, 1, 3)
        k = k.reshape(B, T, HEADS, HEAD_DIM).transpose(0, 2, 1, 3)
        v = v.reshape(B, T, HEADS, HEAD_DIM).transpose(0, 2, 1, 3)
        scale = HEAD_DIM ** (-0.5)
        logits = jnp.einsum('bhqd,bhkd->bhqk', q, k) * scale
        suppress_A_in = 1.0 - mask_A
        suppress_B_in = 1.0 - mask_B
        col_bias = jnp.zeros((HW, T), logits.dtype)
        col_bias = col_bias.at[:, token_indices_A].set((-SUPPRESS * suppress_A_in)[:, None])
        col_bias = col_bias.at[:, token_indices_B].set((-SUPPRESS * suppress_B_in)[:, None])
        logits = logits + col_bias[None, None, :, :]
        probs = jax.nn.softmax(logits, axis=-1)
        out = jnp.einsum('bhqk,bhkd->bhqd', probs, v)
        out = out.transpose(0, 2, 1, 3).reshape(B, HW, HEADS * HEAD_DIM)
        out = out @ Wo + bo
        out = out + residual
        return out

    def _L3_xattn_ref(x, cond, wq, wk, wv, wo, norm_w):
        import jax, jax.numpy as jnp
        import numpy as np
        D_MODEL = 128
        N_HEADS = 16
        N_KV_HEADS = 4
        HEAD_DIM = D_MODEL // N_HEADS
        SPEAKER_DIM = 256
        EPS = 1e-05

        def rmsnorm(x, w, eps=EPS):
            xf = x.astype(jnp.float32)
            inv = jax.lax.rsqrt(jnp.mean(xf * xf, axis=-1, keepdims=True) + eps)
            return (xf * inv).astype(x.dtype) * w
        B, T, _ = x.shape
        S = cond.shape[1]
        n_rep = N_HEADS // N_KV_HEADS
        residual = x
        xn = rmsnorm(x, norm_w)
        q = (xn @ wq).reshape(B, T, N_HEADS, HEAD_DIM)
        k = (cond @ wk).reshape(B, S, N_KV_HEADS, HEAD_DIM)
        v = (cond @ wv).reshape(B, S, N_KV_HEADS, HEAD_DIM)
        qg = q.reshape(B, T, N_KV_HEADS, n_rep, HEAD_DIM)
        scale = 1.0 / np.sqrt(HEAD_DIM).astype(np.float32)
        scores = jnp.einsum('btgrd,bsgd->bgrts', qg, k) * scale
        attn = jax.nn.softmax(scores.astype(jnp.float32), axis=-1).astype(q.dtype)
        out = jnp.einsum('bgrts,bsgd->btgrd', attn, v).reshape(B, T, N_HEADS * HEAD_DIM)
        return residual + out @ wo
    x = _L0_xattn_ref(x, ctx_2048, L0_xattn_wq, L0_xattn_wk, L0_xattn_wv, L0_xattn_wo, L0_xattn_norm_w)
    x = _L1_xattn_ref(x, ctx_2048, mask_S_fk1, mask_S_fk0, L1_xattn_Wq, L1_xattn_Wk, L1_xattn_Wv, L1_xattn_Wo, L1_xattn_bo, L1_xattn_token_indices_A, L1_xattn_token_indices_B)
    x = _L2_xattn_ref(x, ctx_2048, mask_S_fk1, mask_S_fk0, L2_xattn_Wq, L2_xattn_Wk, L2_xattn_Wv, L2_xattn_Wo, L2_xattn_bo, L2_xattn_token_indices_A, L2_xattn_token_indices_B)
    x = _L3_xattn_ref(x, ctx_2048, L3_xattn_wq, L3_xattn_wk, L3_xattn_wv, L3_xattn_wo, L3_xattn_norm_w)
    return x

_drawn_inputs = setup_inputs


def setup_inputs(seed=0):
    import zlib

    import numpy as np

    out = dict(_drawn_inputs(seed))
    spreads = {'L0_xattn_norm_w': (1.0, 0.6),
     'L1_xattn_bo': (0.0, 0.1),
     'L2_xattn_bo': (0.0, 0.1),
     'L3_xattn_norm_w': (1.0, 0.6)}
    factors = {'mask_S_fk1': 8.0,
     'mask_S_fk0': 8.0,
     'L0_xattn_wq': 8.0,
     'L0_xattn_wk': 8.0,
     'L1_xattn_Wq': 8.0,
     'L1_xattn_Wk': 8.0,
     'L2_xattn_Wq': 8.0,
     'L2_xattn_Wk': 8.0,
     'L3_xattn_wq': 8.0,
     'L3_xattn_wk': 8.0}
    for name, (base, spread) in spreads.items():
        noise = np.random.default_rng([zlib.crc32(name.encode()), seed]).standard_normal(out[name].shape)
        drawn = base * np.exp(spread * noise) if base else spread * noise
        out[name] = jnp.asarray(drawn.astype(out[name].dtype))
    for name, factor in factors.items():
        out[name] = (out[name] * factor).astype(out[name].dtype)
    return out
```

```python
from contextlib import ExitStack

import numpy as np

import concourse.bass as bass
from concourse import mybir

ALU = mybir.AluOpType
ACT = mybir.ActivationFunctionType
AX = mybir.AxisListType
F32 = mybir.dt.float32
F32R = mybir.dt.float32r
I32 = mybir.dt.int32

P = 128
B, T, C = 8, 128, 128
S, CT = 128, 256
HEADS = 16
WIDE_D, NARROW_D = 64, 8
KV_HEADS = 4
REP = HEADS // KV_HEADS
INNER = HEADS * WIDE_D
SUPPRESS = 20.0
EPS = 1e-5
PAIR = 2
TURNS = B // PAIR
TOK = PAIR * T
CC = CT // P
IC = INNER // P
BANK = 512
LAYERS = 4
NARROW = (0, 3)
OCTETS = PAIR * 2
STEPS = OCTETS + 2
HUGE = 3.0e38

NQ, NK, NV, NO = 0, 2 * C, 2 * C + 2 * CC * C, 2 * C + 4 * CC * C
NARROW_COLS = NO + 2 * REP * C
WK, WV, WQ, WO = 0, CC * INNER, 2 * CC * INNER, 2 * CC * INNER + INNER
WIDE_COLS = WO + IC * C
STAGE = 2048

BEFORE_MEAN = {0: ["ksm", "vsm"], 1: [], 2: [], 3: []}
BEFORE_Q = {0: ["k1.0", "k1.1"], 1: ["k2.0", "k2.1"], 2: ["v2.2", "v2.3"], 3: []}
AFTER_Q = {0: ["k1.2", "k1.3"], 1: [], 2: [], 3: []}
AFTER_STEP = {
    0: [[], [], ["v1.0"], ["v1.1"], ["v1.2"], ["v1.3"]],
    1: [[], [], [], [], ["k2.2", "k2.3"], ["v2.0", "v2.1"]],
    2: [[], [], [], [], [], []],
    3: [[], [], [], [], [], []],
}


def task_order():
    order = []
    for l in range(LAYERS):
        order += BEFORE_MEAN[l]
        order += [f"mean{l}"] if l in NARROW else []
        order += BEFORE_Q[l]
        order += [f"q{l}.0"] if l in NARROW else [f"q{l}.{j}" for j in range(4)]
        order += AFTER_Q[l]
        for step in AFTER_STEP[l]:
            order += step
        order.append(f"o{l}")
    return order


TASKS = task_order()
assert len(TASKS) % 2 == 0
BANK_TASKS = len(TASKS) // 2
OCTET_USES = LAYERS * OCTETS
O_BANKS = {l: PAIR if l in NARROW else OCTETS for l in range(LAYERS)}
O_FIRST = {l: sum(O_BANKS[m] for m in range(l)) for l in range(LAYERS)}
O_USES = sum(O_BANKS.values()) // 2
DVE_LINKS = 2 + 2 * OCTETS


def build(nc, xT, ctxT, narrow_w, wide_w, vectors, masks, tokens, constants, outT):
    with ExitStack() as ctx:
        def sb(name, shape, dt=F32):
            return ctx.enter_context(nc.sbuf_tensor(name, shape, dt))

        def sem(name):
            return ctx.enter_context(nc.semaphore(name))

        def pair(name):
            return [sem(f"{name}_{i}") for i in range(2)]

        def banks(name):
            return [ctx.enter_context(nc.psum_tensor(f"{name}{i}", [P, BANK], F32)) for i in range(2)]

        scores_ps, pt_ps, o_ps, proj_ps = banks("scores_ps"), banks("pt_ps"), banks("o_ps"), banks("proj_ps")

        wn = sb("wn", [P, NARROW_COLS])
        w_hi = sb("w_hi", [P, 2, WIDE_COLS], F32R)
        w_lo = sb("w_lo", [P, 2, WIDE_COLS], F32R)
        vec = sb("vec", [P, 4])
        consts = sb("consts", [P, P + REP + KV_HEADS])
        mask = sb("mask", [P, 2])
        tok_i = sb("tok_i", [P, 8], I32)
        tok_f = sb("tok_f", [P, 16])
        key_i = sb("key_i", [P, S], I32)
        key_f = sb("key_f", [P, S])
        suppress = sb("suppress", [P, 2])
        hit = sb("hit", [P, 2, S])
        col_bias = sb("col_bias", [P, 3, S])
        mean_w = sb("mean_w", [P, 1])
        half_power = sb("half_power", [P, 1])
        identity = consts[:, 0:P]
        rep_mask = consts[:, P:P + REP]
        group_mask = consts[:, P + REP:]

        x_in = sb("x_in", [P, TOK])
        x = sb("x", [P, TOK])
        x_out = sb("x_out", [P, TOK])
        x_sq = sb("x_sq", [P, TOK])
        rms = sb("rms", [P, PAIR])
        inv_rms = sb("inv_rms", [P, PAIR])
        x_hi = sb("x_hi", [P, TOK], F32R)
        x_lo = sb("x_lo", [P, TOK], F32R)
        c_in = sb("c_in", [P, CC, TOK])
        c_hi = sb("c_hi", [P, CC, TOK], F32R)
        c_lo = sb("c_lo", [P, CC, TOK], F32R)
        kT = {l: sb(f"kT{l}", [P, IC, TOK]) for l in (1, 2)}
        v = {l: sb(f"v{l}", [P, PAIR, INNER]) for l in (1, 2)}
        k_narrow = sb("k_narrow", [P, 2, TOK])
        v_narrow = sb("v_narrow", [P, PAIR, 2, P])
        kd_hi = sb("kd_hi", [P, PAIR, REP, S], F32R)
        kd_lo = sb("kd_lo", [P, PAIR, REP, S], F32R)
        qT = sb("qT", [P, IC, TOK])
        q_narrow = sb("q_narrow", [P, TOK])
        oT_hi = sb("oT_hi", [P, IC, TOK], F32R)
        oT_lo = sb("oT_lo", [P, IC, TOK], F32R)
        qd_hi, qd_lo = oT_hi[:, REP:], oT_lo[:, REP:]
        probs = sb("probs", [P, 2, 2, BANK])
        probsT = sb("probsT", [P, 2, BANK])
        negmax = sb("negmax", [P, 2, 2, 4])
        rowsum = sb("rowsum", [P, 2, 2, 4])
        inv = sb("inv", [P, 2, 2, 4])

        setup_loaded, setup_done = sem("setup_loaded"), sem("setup_done")
        narrow_loaded = sem("narrow_loaded")
        stage_loaded = [sem(f"stage_loaded_{i}") for i in range(4)]
        stage_hi, stage_lo = sem("stage_hi"), sem("stage_lo")
        keys_made, ones_made, setup_step = sem("keys_made"), sem("ones_made"), sem("setup_step")
        x_loaded, c_loaded = sem("x_loaded"), sem("c_loaded")
        c_rounded, c_split = sem("c_rounded"), sem("c_split")
        rms_made = sem("rms_made")
        sq_ready, x_ready = sem("sq_ready"), sem("x_ready")
        proj_full, proj_read = pair("proj_full"), pair("proj_read")
        qd_hi_made, qd_lo_made = sem("qd_hi_made"), sem("qd_lo_made")
        kd_hi_made, kd_lo_made = sem("kd_hi_made"), sem("kd_lo_made")
        scores_full, scores_read = pair("scores_full"), pair("scores_read")
        exps_made, inv_made, probs_made = pair("exps_made"), pair("inv_made"), pair("probs_made")
        pt_full, pt_read = pair("pt_full"), pair("pt_read")
        o_full, o_read = pair("o_full"), pair("o_read")
        dve_link = sem("dve_link")
        out_stored = sem("out_stored")
        passed = {e: sem(f"passed_{e}") for e in ("sp", "pool", "dve")}

        stages = [kT[1][:].rearrange("p a b -> p (a b)"), v[1][:].rearrange("p a b -> p (a b)"),
                  kT[2][:].rearrange("p a b -> p (a b)"), v[2][:].rearrange("p a b -> p (a b)")]
        loads = [(w, n) for w in range(2) for n in range(WIDE_COLS // STAGE)]

        block = ctx.enter_context(nc.Block())

        def task(name):
            n = TASKS.index(name)
            return n % 2, n // 2

        @block.sync
        def _(sp):
            sp.dma_start(wn[:], narrow_w).then_inc(narrow_loaded, 16)
            sp.dma_start(consts[:], constants).then_inc(setup_loaded, 16)
            sp.dma_start(vec[:], vectors).then_inc(setup_loaded, 16)
            sp.dma_start(mask[:], masks).then_inc(setup_loaded, 16)
            sp.dma_start(tok_i[:], tokens.broadcast_to([P, 8])).then_inc(setup_loaded, 16)
            for n, (w, c) in enumerate(loads):
                if n >= 4:
                    sp.wait_ge(stage_lo, n - 3)
                sp.dma_start(stages[n % 4], wide_w[:, w, c * STAGE:(c + 1) * STAGE]).then_inc(stage_loaded[n % 4], 16)
            sp.dma_start(x_in[:], xT[:, 0:TOK]).then_inc(x_loaded, 16)
            sp.dma_start(c_in[:], ctxT[:, :, 0:TOK]).then_inc(c_loaded, 16)

            def store(i):
                bank, use = task("o3")
                sp.wait_ge(proj_read[bank], BANK_TASKS * i + use + 1)
                sp.sem_inc(passed["sp"], 1)
                sp.dma_start(outT[:, bass.ds(i * TOK, TOK)], x_out[:]).then_inc(out_stored, 16)

            with sp.Fori(0, TURNS - 1) as i:
                sp.wait_ge(c_split, i + 1)
                bank, use = task("vsm")
                sp.wait_ge(proj_read[bank], BANK_TASKS * i + use + 1)
                sp.sem_inc(passed["sp"], 1)
                sp.dma_start(c_in[:], ctxT[:, :, bass.ds(i * TOK + TOK, TOK)]).then_inc(c_loaded, 16)
                bank, use = task("o0")
                sp.wait_ge(proj_read[bank], BANK_TASKS * i + use + 1)
                sp.sem_inc(passed["sp"], 1)
                sp.dma_start(x_in[:], xT[:, bass.ds(i * TOK + TOK, TOK)]).then_inc(x_loaded, 16)
                store(i)
            store(TURNS - 1)
            sp.wait_ge(out_stored, 16 * TURNS)

        @block.gpsimd
        def _(pool):
            nc.gpsimd.memset(half_power[:], -0.5)
            nc.gpsimd.memset(mean_w[:], 1.0 / C).then_inc(ones_made, 1)
            nc.gpsimd.iota(key_i[:], pattern=[[1, S]], base=0, channel_multiplier=0).then_inc(keys_made, 1)
            with pool.Fori(0, TURNS) as i:
                pool.wait_ge(c_loaded, 16 * i + 16)
                pool.sem_inc(passed["pool"], 1)
                nc.gpsimd.tensor_copy(c_hi[:], c_in[:]).then_inc(c_rounded, 1)
                pool.wait_ge(c_rounded, i + 1)
                nc.gpsimd.tensor_tensor(c_lo[:], c_in[:], c_hi[:].bitcast(F32), ALU.subtract).then_inc(c_split, 1)
                for n in range(OCTET_USES):
                    if n % OCTETS == 0 and n // OCTETS in NARROW:
                        l = n // OCTETS
                        bank, use = task(f"mean{l}")
                        pool.wait_ge(proj_read[bank], BANK_TASKS * i + use + 1)
                        nc.gpsimd.tensor_tensor(inv_rms[:], rms[:], half_power[:].broadcast_to([P, PAIR]),
                                                ALU.pow).then_inc(rms_made, 1)
                    for side in range(2):
                        pool.wait_ge(inv_made[side], OCTET_USES * i + n + 1)
                        p4 = probs[:, n % 2, side, :].rearrange("p (h k) -> p h k", h=4)
                        nc.gpsimd.tensor_tensor(
                            p4, p4, inv[:, n % 2, side, :].unsqueeze(2).broadcast_to([P, 4, S]), ALU.mult,
                        ).then_inc(probs_made[side], 1)

        @block.scalar
        def _(act):
            for n, (w, c) in enumerate(loads):
                act.wait_ge(stage_loaded[n % 4], 16 * (n // 4 + 1))
                nc.scalar.activation(w_hi[:, w, c * STAGE:(c + 1) * STAGE], stages[n % 4],
                                     ACT.Copy).then_inc(stage_hi, 1)
            act.wait_ge(setup_loaded, 16 * 4)
            act.wait_ge(setup_done, 1)
            act.wait_ge(stage_lo, len(loads))
            with act.Fori(0, TURNS) as i:
                def from_bank(name, dst, scale=1.0, cols=BANK):
                    bank, use = task(name)
                    act.wait_ge(proj_full[bank], BANK_TASKS * i + use + 1)
                    nc.scalar.activation(dst, proj_ps[bank][:, 0:cols], ACT.Copy,
                                         scale=scale).then_inc(proj_read[bank], 1)

                def fill(name):
                    if name == "ksm":
                        from_bank(name, k_narrow[:].rearrange("p l t -> p (l t)"))
                        diagonal_keys(0)
                    elif name == "vsm":
                        from_bank(name, v_narrow[:].rearrange("p b l n -> p (b l n)"))
                    elif name[0] == "k":
                        l, j = int(name[1]), int(name[3])
                        from_bank(name, kT[l][:, 2 * j:2 * j + 2, :].rearrange("p c t -> p (c t)"))
                    else:
                        l, j = int(name[1]), int(name[3])
                        from_bank(name, v[l][:, j // 2, j % 2 * BANK:(j % 2 + 1) * BANK])

                def diagonal_keys(n):
                    bank, use = task("ksm")
                    act.wait_ge(proj_read[bank], BANK_TASKS * i + use + 1)
                    for r in range(REP):
                        nc.scalar.activation(
                            kd_hi[:, :, r, :], k_narrow[:, n, :].rearrange("p (b k) -> p b k", b=PAIR),
                            ACT.Copy, scale=rep_mask[:, r:r + 1]).then_inc(kd_hi_made, 1)

                for l in range(LAYERS):
                    for name in BEFORE_MEAN[l] + BEFORE_Q[l]:
                        fill(name)
                    if l in NARROW:
                        from_bank(f"q{l}.0", q_narrow[:], scale=-float(1.0 / np.sqrt(np.float32(NARROW_D))), cols=TOK)
                        bank, use = task(f"q{l}.0")
                        act.wait_ge(proj_read[bank], BANK_TASKS * i + use + 1)
                        for g in range(KV_HEADS):
                            nc.scalar.activation(qd_hi[:, g, :], q_narrow[:], ACT.Copy,
                                                 scale=group_mask[:, g:g + 1]).then_inc(qd_hi_made, 1)
                    else:
                        for j in range(4):
                            from_bank(f"q{l}.{j}", qT[:, 2 * j:2 * j + 2, :].rearrange("p c t -> p (c t)"),
                                      scale=-WIDE_D ** -0.5)
                    for name in AFTER_Q[l]:
                        fill(name)
                    for s in range(STEPS):
                        if s < OCTETS:
                            n = OCTETS * l + s
                            for side in range(2):
                                act.wait_ge(scores_read[side], OCTET_USES * i + n + 1)
                                for h in range(4):
                                    e = probs[:, n % 2, side, h * S:(h + 1) * S]
                                    last = nc.scalar.activation(
                                        e, e, ACT.Exp, scale=-1.0, bias=negmax[:, n % 2, side, h:h + 1],
                                        accum_out=rowsum[:, n % 2, side, h:h + 1])
                                last.then_inc(exps_made[side], 1)
                        if l == 1 and s == OCTETS:
                            diagonal_keys(1)
                        for name in AFTER_STEP[l][s]:
                            fill(name)

        @block.vector
        def _(dve):
            steps = [0]

            def setup(ins):
                steps[0] += 1
                ins.then_inc(setup_step, 1)
                dve.wait_ge(setup_step, steps[0])

            nc.vector.memset(col_bias[:, 2, :], 0.0)
            dve.wait_ge(setup_loaded, 16 * 4)
            dve.wait_ge(keys_made, 1)
            dve.wait_ge(narrow_loaded, 16)
            for n in range(2):
                wq = wn[:, NQ + n * C:NQ + (n + 1) * C]
                setup(nc.vector.tensor_scalar(wq, wq, vec[:, n:n + 1], None, ALU.mult))
            setup(nc.vector.tensor_copy(key_f[:], key_i[:]))
            setup(nc.vector.tensor_copy(tok_f[:, 0:8], tok_i[:]))
            setup(nc.vector.tensor_scalar(tok_f[:, 8:16], tok_f[:, 0:8], float(S), None, ALU.add))
            setup(nc.vector.tensor_scalar(suppress[:], mask[:], -SUPPRESS, SUPPRESS, ALU.mult, ALU.add))
            for l in range(2):
                for m in range(2):
                    first = 4 * l + 2 * m
                    setup(nc.vector.tensor_scalar(hit[:, m, :], key_f[:], tok_f[:, first:first + 1], None,
                                                  ALU.is_equal))
                    for t in (first + 1, first + 8, first + 9):
                        setup(nc.vector.scalar_tensor_tensor(
                            out=hit[:, m, :], in0=key_f[:], scalar=tok_f[:, t:t + 1], in1=hit[:, m, :],
                            op0=ALU.is_equal, op1=ALU.max))
                setup(nc.vector.tensor_scalar(col_bias[:, l, :], hit[:, 1, :], -1.0, 1.0, ALU.mult, ALU.add))
                setup(nc.vector.tensor_tensor(hit[:, 0, :], hit[:, 0, :], col_bias[:, l, :], ALU.mult))
                setup(nc.vector.tensor_scalar(hit[:, 1, :], hit[:, 1, :], suppress[:, 1:2], None, ALU.mult))
                setup(nc.vector.scalar_tensor_tensor(
                    out=col_bias[:, l, :], in0=hit[:, 0, :], scalar=suppress[:, 0:1], in1=hit[:, 1, :],
                    op0=ALU.mult, op1=ALU.add))
            nc.vector.memset(x_sq[:], 0.0).then_inc(setup_done, 1)
            for n, (w, c) in enumerate(loads):
                dve.wait_ge(stage_hi, n + 1)
                cols = slice(c * STAGE, (c + 1) * STAGE)
                nc.vector.tensor_tensor(w_lo[:, w, cols], stages[n % 4], w_hi[:, w, cols].bitcast(F32),
                                        ALU.subtract).then_inc(stage_lo, 1)
            with dve.Fori(0, TURNS) as i:
                links = [0]

                def link(ins):
                    links[0] += 1
                    ins.then_inc(dve_link, 1)
                    dve.wait_ge(dve_link, DVE_LINKS * i + links[0])

                def square(src):
                    nc.vector.tensor_tensor(x_sq[:], src, src, ALU.mult).then_inc(sq_ready, 1)

                def mean_out(l):
                    bank, use = task(f"mean{l}")
                    dve.wait_ge(proj_full[bank], BANK_TASKS * i + use + 1)
                    nc.vector.tensor_scalar(rms[:], proj_ps[bank][:, 0:PAIR], EPS, None,
                                            ALU.add).then_inc(proj_read[bank], 1)

                def split_x():
                    link(nc.vector.tensor_copy(x_hi[:], x[:]))
                    nc.vector.tensor_tensor(x_lo[:], x[:], x_hi[:].bitcast(F32), ALU.subtract).then_inc(x_ready, 1)

                def diagonal_keys(n):
                    for r in range(REP):
                        dve.wait_ge(kd_hi_made, 2 * REP * i + REP * n + r + 1)
                        nc.vector.scalar_tensor_tensor(
                            out=kd_lo[:, :, r, :], in0=k_narrow[:, n, :].rearrange("p (b k) -> p b k", b=PAIR),
                            scalar=rep_mask[:, r:r + 1], in1=kd_hi[:, :, r, :].bitcast(F32),
                            op0=ALU.mult, op1=ALU.subtract).then_inc(kd_lo_made, 1)

                for l in range(LAYERS):
                    if l == 0:
                        dve.wait_ge(x_loaded, 16 * i + 16)
                        square(x_in[:])
                    if l in NARROW:
                        mean_out(l)
                        if l == 0:
                            diagonal_keys(0)
                        for g in range(KV_HEADS):
                            dve.wait_ge(qd_hi_made, KV_HEADS * (2 * i + NARROW.index(l)) + g + 1)
                            nc.vector.scalar_tensor_tensor(
                                out=qd_lo[:, g, :], in0=q_narrow[:], scalar=group_mask[:, g:g + 1],
                                in1=qd_hi[:, g, :].bitcast(F32), op0=ALU.mult,
                                op1=ALU.subtract).then_inc(qd_lo_made, 1)
                    for s in range(STEPS):
                        if s >= 2:
                            n = OCTETS * l + s - 2
                            for side in range(2):
                                dve.wait_ge(pt_full[side], OCTET_USES * i + n + 1)
                                nc.vector.tensor_copy(probsT[:, side, :], pt_ps[side][:]).then_inc(pt_read[side], 1)
                        if 1 <= s <= OCTETS:
                            n = OCTETS * l + s - 1
                            for side in range(2):
                                dve.wait_ge(exps_made[side], OCTET_USES * i + n + 1)
                                nc.vector.reciprocal(inv[:, n % 2, side, :],
                                                     rowsum[:, n % 2, side, :]).then_inc(inv_made[side], 1)
                        if s < OCTETS:
                            n = OCTETS * l + s
                            bias = col_bias[:, 2 if l in NARROW else l - 1, :]
                            scale = inv_rms[:, s // 2:s // 2 + 1] if l in NARROW else 1.0
                            if l in NARROW and s == 0:
                                dve.wait_ge(rms_made, 2 * i + NARROW.index(l) + 1)
                                dve.sem_inc(passed["dve"], 1)
                            for side in range(2):
                                dve.wait_ge(scores_full[side], OCTET_USES * i + n + 1)
                                dve.sem_inc(passed["dve"], 1)
                                for h in range(4):
                                    cols = slice(h * S, (h + 1) * S)
                                    last = nc.vector.tensor_tensor_reduce(
                                        out=probs[:, n % 2, side, cols], in0=scores_ps[side][:, cols], in1=bias,
                                        scale=scale, scalar=HUGE, op0=ALU.add, op1=ALU.min,
                                        accum_out=negmax[:, n % 2, side, h:h + 1])
                                last.then_inc(scores_read[side], 1)
                        if s >= 2:
                            o = s - 2
                            if l in NARROW and o % 2 == 1:
                                m = O_FIRST[l] + o // 2
                                b = o // 2
                                dve.wait_ge(o_full[m % 2], O_USES * i + m // 2 + 1)
                                nc.vector.tensor_copy(
                                    qT[:, 0:REP, b * T:(b + 1) * T],
                                    o_ps[m % 2][:].rearrange("p (r q) -> p r q", r=REP)).then_inc(o_read[m % 2], 1)
                            if l not in NARROW:
                                m = O_FIRST[l] + o
                                b, half = o // 2, o % 2
                                src = o_ps[m % 2][:].rearrange("p (c q) -> p c q", c=4)
                                hi = oT_hi[:, 4 * half:4 * half + 4, b * T:(b + 1) * T]
                                dve.wait_ge(o_full[m % 2], O_USES * i + m // 2 + 1)
                                link(nc.vector.tensor_copy(hi, src))
                                nc.vector.tensor_tensor(
                                    oT_lo[:, 4 * half:4 * half + 4, b * T:(b + 1) * T], src, hi.bitcast(F32),
                                    ALU.subtract).then_inc(o_read[m % 2], 1)
                        if l == 1 and s == OCTETS:
                            diagonal_keys(1)
                    bank, use = task(f"o{l}")
                    dve.wait_ge(proj_full[bank], BANK_TASKS * i + use + 1)
                    y = proj_ps[bank][:, 0:TOK]
                    if l == 0:
                        ins = nc.vector.tensor_tensor(x[:], y, x_in[:], ALU.add)
                    elif l < 3:
                        ins = nc.vector.scalar_tensor_tensor(out=x[:], in0=y, scalar=vec[:, l + 1:l + 2], in1=x[:],
                                                             op0=ALU.add, op1=ALU.add)
                    else:
                        dve.wait_ge(out_stored, 16 * i)
                        ins = nc.vector.tensor_tensor(x_out[:], y, x[:], ALU.add)
                    ins.then_inc(proj_read[bank], 1)
                    dve.wait_ge(proj_read[bank], BANK_TASKS * i + use + 1)
                    if l < 2:
                        split_x()
                    elif l == 2:
                        square(x[:])

        @block.tensor
        def _(pe):
            pe.wait_ge(narrow_loaded, 16)
            pe.wait_ge(setup_loaded, 16 * 4)
            pe.wait_ge(setup_done, 1)
            pe.wait_ge(ones_made, 1)
            with pe.Fori(0, TURNS) as i:
                def bank_of(name):
                    bank, use = task(name)
                    pe.wait_ge(proj_read[bank], BANK_TASKS * i + use)
                    return bank

                def three(out, stationary, moving):
                    products = [(a, b) for a, b in zip(stationary, moving)]
                    for n, ((a_hi, a_lo), (b_hi, b_lo)) in enumerate(products):
                        nc.tensor.matmul(out, a_hi, b_hi, start=(n == 0), stop=False)
                        nc.tensor.matmul(out, a_lo, b_hi, start=False, stop=False)
                        last = nc.tensor.matmul(out, a_hi, b_lo, start=False, stop=(n == len(products) - 1))
                    return last

                def both(first, w, cols):
                    return w_hi[:, w, first:first + cols], w_lo[:, w, first:first + cols]

                def project_context(name):
                    bank = bank_of(name)
                    out = proj_ps[bank]
                    if name == "ksm":
                        pe.wait_ge(c_loaded, 16 * i + 16)
                        for n in range(2):
                            for c in range(CC):
                                first = NK + (n * CC + c) * C
                                last = nc.tensor.matmul(out[:, n * TOK:(n + 1) * TOK], wn[:, first:first + C],
                                                        c_in[:, c, :], start=(c == 0), stop=(c == CC - 1))
                    elif name == "vsm":
                        for b in range(PAIR):
                            for c in range(CC):
                                first = NV + c * 2 * C
                                last = nc.tensor.matmul(out[:, b * 2 * C:(b + 1) * 2 * C],
                                                        c_in[:, c, b * S:(b + 1) * S], wn[:, first:first + 2 * C],
                                                        start=(c == 0), stop=(c == CC - 1))
                    else:
                        pe.wait_ge(c_split, i + 1)
                        l, j = int(name[1]), int(name[3])
                        if name[0] == "k":
                            for n in range(2):
                                chunk = 2 * j + n
                                last = three(out[:, n * TOK:(n + 1) * TOK],
                                             [both(WK + c * INNER + chunk * P, l - 1, P) for c in range(CC)],
                                             [(c_hi[:, c, :], c_lo[:, c, :]) for c in range(CC)])
                        else:
                            b, n = j // 2, j % 2
                            keys = slice(b * S, (b + 1) * S)
                            last = three(out[:, :],
                                         [(c_hi[:, c, keys], c_lo[:, c, keys]) for c in range(CC)],
                                         [both(WV + c * INNER + n * BANK, l - 1, BANK) for c in range(CC)])
                    last.then_inc(proj_full[bank], 1)

                def mean_of_squares(l):
                    pe.wait_ge(sq_ready, 2 * i + NARROW.index(l) + 1)
                    bank = bank_of(f"mean{l}")
                    for b in range(PAIR):
                        last = nc.tensor.matmul(proj_ps[bank][:, b:b + 1], x_sq[:, b * T:(b + 1) * T], mean_w[:],
                                                start=True, stop=True)
                    last.then_inc(proj_full[bank], 1)

                def queries(l):
                    if l in NARROW:
                        bank = bank_of(f"q{l}.0")
                        first = NQ + NARROW.index(l) * C
                        nc.tensor.matmul(proj_ps[bank][:, 0:TOK], wn[:, first:first + C],
                                         (x_in if l == 0 else x)[:], start=True,
                                         stop=True).then_inc(proj_full[bank], 1)
                        return
                    pe.wait_ge(x_ready, 2 * i + l)
                    for j in range(4):
                        bank = bank_of(f"q{l}.{j}")
                        for n in range(2):
                            last = three(proj_ps[bank][:, n * TOK:(n + 1) * TOK],
                                         [both(WQ + (2 * j + n) * P, l - 1, P)], [(x_hi[:], x_lo[:])])
                        last.then_inc(proj_full[bank], 1)

                def read_out(names):
                    latest = {}
                    for name in names:
                        bank, use = task(name)
                        latest[bank] = max(latest.get(bank, 0), use + 1)
                    for bank, use in latest.items():
                        pe.wait_ge(proj_read[bank], BANK_TASKS * i + use)

                def scores(l, o):
                    n = OCTETS * l + o
                    b, half = o // 2, o % 2
                    seq = slice(b * T, (b + 1) * T)
                    for side in range(2):
                        pe.wait_ge(scores_read[side], OCTET_USES * i + n)
                    if l in NARROW:
                        m = NARROW.index(l)
                        pe.wait_ge(kd_lo_made, REP * (2 * i + m) + REP)
                        for side in range(2):
                            g = 2 * half + side
                            pe.wait_ge(qd_lo_made, KV_HEADS * (2 * i + m) + g + 1)
                            three(scores_ps[side][:], [(qd_hi[:, g, seq], qd_lo[:, g, seq])],
                                  [(kd_hi[:, b].rearrange("p r k -> p (r k)"),
                                    kd_lo[:, b].rearrange("p r k -> p (r k)"))]).then_inc(scores_full[side], 1)
                        return
                    read_out([f"k{l}.{j}" for j in range(4)] + [f"q{l}.{2 * half + j}" for j in range(2)])
                    for h in range(4):
                        for side in range(2):
                            rows = slice(side * WIDE_D, (side + 1) * WIDE_D)
                            last = nc.tensor.matmul(scores_ps[side][:, h * S:(h + 1) * S],
                                                    qT[rows, 4 * half + h, seq], kT[l][rows, 4 * half + h, seq],
                                                    start=True, stop=True)
                            if h == 3:
                                last.then_inc(scores_full[side], 1)

                def transpose_probs(l, o):
                    n = OCTETS * l + o
                    for side in range(2):
                        pe.wait_ge(probs_made[side], OCTET_USES * i + n + 1)
                        pe.wait_ge(pt_read[side], OCTET_USES * i + n)
                        for h in range(4):
                            cols = slice(h * S, (h + 1) * S)
                            last = nc.tensor.transpose(pt_ps[side][:, cols], probs[:, n % 2, side, cols], identity)
                        last.then_inc(pt_full[side], 1)

                def weighted_values(l, o):
                    n = OCTETS * l + o
                    b, half = o // 2, o % 2
                    m = O_FIRST[l] + (o // 2 if l in NARROW else o)
                    if l in NARROW:
                        if half == 0:
                            pe.wait_ge(o_read[m % 2], O_USES * i + m // 2)
                        if o == 0:
                            read_out(["vsm"])
                        for side in range(2):
                            g = 2 * half + side
                            pe.wait_ge(pt_read[side], OCTET_USES * i + n + 1)
                            last = nc.tensor.matmul(o_ps[m % 2][32 * g:32 * g + 32, :],
                                                    v_narrow[:, b, NARROW.index(l), 32 * g:32 * g + 32],
                                                    probsT[:, side, :], start=True, stop=True)
                        if half == 1:
                            last.then_inc(o_full[m % 2], 1)
                        return
                    pe.wait_ge(o_read[m % 2], O_USES * i + m // 2)
                    if o == 0:
                        read_out([f"v{l}.{j}" for j in range(4)])
                    for side in range(2):
                        pe.wait_ge(pt_read[side], OCTET_USES * i + n + 1)
                    for h in range(4):
                        for side in range(2):
                            head = 8 * half + 2 * h + side
                            last = nc.tensor.matmul(
                                o_ps[m % 2][side * WIDE_D:(side + 1) * WIDE_D, h * T:(h + 1) * T],
                                v[l][:, b, head * WIDE_D:(head + 1) * WIDE_D], probsT[:, side, h * T:(h + 1) * T],
                                start=True, stop=True)
                    last.then_inc(o_full[m % 2], 1)

                def output_projection(l):
                    bank = bank_of(f"o{l}")
                    for m in range(O_FIRST[l] + O_BANKS[l] - 2, O_FIRST[l] + O_BANKS[l]):
                        pe.wait_ge(o_read[m % 2], O_USES * i + m // 2 + 1)
                    if l in NARROW:
                        for r in range(REP):
                            first = NO + (NARROW.index(l) * REP + r) * C
                            last = nc.tensor.matmul(proj_ps[bank][:, 0:TOK], wn[:, first:first + C], qT[:, r, :],
                                                    start=(r == 0), stop=(r == REP - 1))
                    else:
                        last = three(proj_ps[bank][:, 0:TOK], [both(WO + c * C, l - 1, C) for c in range(IC)],
                                     [(oT_hi[:, c, :], oT_lo[:, c, :]) for c in range(IC)])
                    last.then_inc(proj_full[bank], 1)

                for l in range(LAYERS):
                    for name in BEFORE_MEAN[l]:
                        project_context(name)
                    if l in NARROW:
                        mean_of_squares(l)
                    for name in BEFORE_Q[l]:
                        project_context(name)
                    queries(l)
                    for name in AFTER_Q[l]:
                        project_context(name)
                    for s in range(STEPS):
                        if s >= 2:
                            transpose_probs(l, s - 2)
                        if s < OCTETS:
                            scores(l, s)
                        if s >= 2:
                            weighted_values(l, s - 2)
                        for name in AFTER_STEP[l][s]:
                            project_context(name)
                    output_projection(l)


def kernel(**inputs):
    from concourse import bacc
    from concourse.bass_utils import run_bass_kernel_spmd

    a = {k: np.ascontiguousarray(x) for k, x in inputs.items()}

    def chunks(w):
        return w.reshape(-1, P, w.shape[1]).transpose(1, 0, 2).reshape(P, -1)

    def narrow_keys(w):
        w = np.repeat(w.reshape(CT, KV_HEADS, 1, NARROW_D), REP, axis=2)
        return chunks(w.reshape(CT, P))

    def narrow_values(w):
        out = np.zeros((CT, KV_HEADS, 32), w.dtype)
        out[:, :, :NARROW_D] = w.reshape(CT, KV_HEADS, NARROW_D)
        return out.reshape(CC, P, 1, P)

    def narrow_out(w):
        out = np.zeros((KV_HEADS, 32, REP, C), w.dtype)
        out[:, :NARROW_D] = w.reshape(KV_HEADS, REP, NARROW_D, C).transpose(0, 2, 1, 3)
        return out.reshape(P, REP * C)

    narrow_v = np.concatenate([narrow_values(a[f"L{l}_xattn_wv"]) for l in NARROW], axis=2)
    narrow_w = np.concatenate(
        [a[f"L{l}_xattn_wq"] for l in NARROW] + [narrow_keys(a[f"L{l}_xattn_wk"]) for l in NARROW]
        + [narrow_v.transpose(1, 0, 2, 3).reshape(P, -1)] + [narrow_out(a[f"L{l}_xattn_wo"]) for l in NARROW], axis=1)
    wide_w = np.stack([np.concatenate([chunks(a[f"L{l}_xattn_{w}"]) for w in ("Wk", "Wv", "Wq", "Wo")], axis=1)
                       for l in (1, 2)], axis=1)
    vectors = np.stack([a["L0_xattn_norm_w"], a["L3_xattn_norm_w"], a["L1_xattn_bo"], a["L2_xattn_bo"]], axis=1)
    masks = np.stack([a["mask_S_fk1"], a["mask_S_fk0"]], axis=1)
    tokens = np.concatenate([a[f"L{l}_xattn_token_indices_{m}"] for l in (1, 2) for m in "AB"])[None, :]
    if tokens.dtype.itemsize == 8:
        tokens = tokens.view(np.int32)[:, ::2]
    row = np.arange(P)
    constants = np.concatenate([np.eye(P), row[:, None] // NARROW_D % REP == np.arange(REP),
                                row[:, None] // (NARROW_D * REP) == np.arange(KV_HEADS)], axis=1)
    arrays = {
        "xT": a["x"].reshape(B * T, C).T,
        "ctxT": a["ctx_2048"].reshape(B * S, CC, P).transpose(2, 1, 0),
        "narrow_w": narrow_w, "wide_w": wide_w, "vectors": vectors, "masks": masks, "tokens": tokens,
        "constants": constants.astype(np.float32),
    }
    nc = bacc.Bacc("TRN2", target_bir_lowering=False, num_devices=1)
    arrays = {f"in_{k}": np.ascontiguousarray(x) for k, x in arrays.items()}
    args = [nc.dram_tensor(k, x.shape, mybir.dt.from_np(x.dtype), kind="ExternalInput").ap()
            for k, x in arrays.items()]
    args.append(nc.dram_tensor("outT", (C, B * T), F32, kind="ExternalOutput").ap())
    build(nc, *args)
    r = run_bass_kernel_spmd(nc, [arrays], core_ids=[0])
    return np.ascontiguousarray(r.results[0]["outT"].T).reshape(B, T, C)
```

```python
from contextlib import ExitStack

import numpy as np

import concourse.bass as bass
from concourse import mybir

ALU = mybir.AluOpType
ACT = mybir.ActivationFunctionType
F32 = mybir.dt.float32
F32R = mybir.dt.float32r
I32 = mybir.dt.int32

P = 128
B, T, C = 8, 128, 128
S, CT = 128, 256
HEADS = 16
WIDE_D, NARROW_D = 64, 8
KV_HEADS = 4
REP = HEADS // KV_HEADS
INNER = HEADS * WIDE_D
SUPPRESS = 20.0
EPS = 1e-5
STREAMS = 2
TURNS = B // STREAMS
TOK = STREAMS * T
CC = CT // P
IC = INNER // P
BANK = 512
LAYERS = 4
NARROW = (0, 3)
OCTETS = LAYERS * STREAMS * 2
HUGE = 3.0e38
FREE = 1

NQ, NK, NV, NO = 0, 2 * C, 2 * C + 2 * CC * C, 2 * C + 4 * CC * C
NARROW_COLS = NO + 2 * REP * C
WK, WV = 0, CC * INNER
KV_COLS = 2 * CC * INNER
WQ, WO = 0, INNER
QO_COLS = INNER + IC * C
STAGE = 1024
STAGES = 4

SLOTS = 6
LAG = 3
TURN_SLOTS = SLOTS * LAYERS
FILL = {
    3: ["k2.0"], 4: ["k2.1"], 5: ["k2.2"], 6: ["k2.3"], 7: ["v2.0"], 8: ["v2.1"], 10: ["v2.2"], 12: ["v2.3"],
    17: ["+kn"], 18: ["+k1.0"], 19: ["+k1.1"], 20: ["+k1.2"], 21: ["+k1.3"],
    22: ["+v1.0"], 23: ["+v1.1"], 24: ["+v1.2"], 25: ["+v1.3"], 26: ["+vn"],
}
LOOP_FILL = [name for slot in sorted(FILL) for name in FILL[slot]]
EARLY = [name[1:] for name in LOOP_FILL if name[0] == "+"]
FILL_ORDER = EARLY + [name for name in LOOP_FILL if name[0] != "+"]
SPLIT_SLOT = 14
KEYS3_SLOT, KEYS0_SLOT = 3, 17


def octet(l, b, h):
    return 4 * l + 2 * b + h


O_USES = [(l, what) for l in range(LAYERS) for what in (("pv", "o") if l in NARROW else ("pv0", "pv1", "o"))]
Q_USES = [(l, b, part) for l in range(LAYERS) for b in range(STREAMS) for part in ((0,) if l in NARROW else (0, 1))]


def slot_work(i, last):
    for slot in range(LAG, TURN_SLOTS + LAG):
        front = slot % SLOTS // 3
        back = 1 - front
        n = slot - LAG * front
        front_at = (i, n // SLOTS) if n < TURN_SLOTS else None if last else (i + 1, 0)
        back_at = (i, (slot - LAG * back) // SLOTS)
        fill = [(i + 1, name[1:]) if name[0] == "+" else (i, name) for name in FILL.get(slot, [])
                if not (last and name[0] == "+")]
        yield slot, slot % 3, front, front_at, back, back_at, fill


def build(nc, xT, ctxT, narrow_w, kv_w, qo_w, vectors, masks, tokens, constants, outT):
    with ExitStack() as ctx:
        def sb(name, shape, dt=F32):
            return ctx.enter_context(nc.sbuf_tensor(name, shape, dt))

        def sem(name):
            return ctx.enter_context(nc.semaphore(name))

        def pair(name):
            return [sem(f"{name}_{i}") for i in range(2)]

        def bank(name):
            return ctx.enter_context(nc.psum_tensor(name, [P, BANK], F32))

        scores_ps = [bank(f"scores_ps{i}") for i in range(2)]
        pt_ps = [bank(f"pt_ps{i}") for i in range(2)]
        o_ps = [bank(f"o_ps{i}") for i in range(2)]
        q_ps, fill_ps = bank("q_ps"), bank("fill_ps")

        wn = sb("wn", [P, NARROW_COLS])
        w_qo = sb("w_qo", [P, 2, QO_COLS])
        w_hi = sb("w_hi", [P, 2, KV_COLS], F32R)
        w_lo = sb("w_lo", [P, 2, KV_COLS], F32R)
        vec = sb("vec", [P, 4])
        consts = sb("consts", [P, P + REP + KV_HEADS])
        identity = consts[:, 0:P]
        rep_mask = consts[:, P:P + REP]
        group_mask = consts[:, P + REP:]
        mask = sb("mask", [P, 2])
        tok_i = sb("tok_i", [P, 8], I32)
        tok_f = sb("tok_f", [P, 16])
        key_i = sb("key_i", [P, S], I32)
        key_f = sb("key_f", [P, S])
        suppress = sb("suppress", [P, 2])
        hit = sb("hit", [P, 2, S])
        col_bias = sb("col_bias", [P, 3, S])
        mean_w = sb("mean_w", [P, P])
        half_power = sb("half_power", [P, 1])

        x_in = sb("x_in", [P, STREAMS, T])
        x = sb("x", [P, STREAMS, T])
        x_out = sb("x_out", [P, STREAMS, T])
        x_sq = sb("x_sq", [P, STREAMS, T])
        rms = sb("rms", [P, STREAMS])
        inv_rms = sb("inv_rms", [P, STREAMS])
        c_in = sb("c_in", [P, CC, TOK])
        c_hi = sb("c_hi", [P, CC, TOK], F32R)
        c_lo = sb("c_lo", [P, CC, TOK], F32R)
        kT = {l: sb(f"kT{l}", [P, IC, TOK]) for l in (1, 2)}
        v = {l: sb(f"v{l}", [P, STREAMS, INNER]) for l in (1, 2)}
        k_narrow = sb("k_narrow", [P, 2, TOK])
        v_narrow = sb("v_narrow", [P, STREAMS, 2, P])
        k_diag = sb("k_diag", [P, STREAMS, REP, S])
        kd_hi = {l: sb(f"kd_hi{l}", [P, STREAMS, REP, S], F32R) for l in NARROW}
        kd_lo = {l: sb(f"kd_lo{l}", [P, STREAMS, REP, S], F32R) for l in NARROW}
        qT = sb("qT", [P, IC, STREAMS, T])
        q_group = sb("q_group", [P, KV_HEADS, T])
        qg_hi = sb("qg_hi", [P, KV_HEADS, T], F32R)
        qg_lo = sb("qg_lo", [P, KV_HEADS, T], F32R)
        oT = sb("oT", [P, IC, STREAMS, T])
        probs = sb("probs", [P, 2, 2, BANK])
        probsT = sb("probsT", [P, 2, BANK])
        negmax = sb("negmax", [P, 2, 2, 4])
        rowsum = sb("rowsum", [P, 2, 2, 4])
        inv = sb("inv", [P, 2, 2, 4])

        setup_loaded, setup_done, narrow_loaded, qo_loaded = (
            sem("setup_loaded"), sem("setup_done"), sem("narrow_loaded"), sem("qo_loaded"))
        stage_loaded = [sem(f"stage_loaded_{i}") for i in range(STAGES)]
        stage_hi, stage_lo = sem("stage_hi"), sem("stage_lo")
        keys_made, ones_made, setup_step = sem("keys_made"), sem("ones_made"), sem("setup_step")
        x_loaded, c_loaded, out_stored = sem("x_loaded"), sem("c_loaded"), pair("out_stored")
        c_rounded, c_split = sem("c_rounded"), sem("c_split")
        sq_ready, rms_out, rms_made = sem("sq_ready"), sem("rms_out"), sem("rms_made")
        fill_full, fill_read = sem("fill_full"), sem("fill_read")
        q_full, q_read = sem("q_full"), sem("q_read")
        qg_made, qg_hi_made, qg_lo_made = sem("qg_made"), sem("qg_hi_made"), sem("qg_lo_made")
        k_diag_made, kd_hi_made, kd_lo_made = sem("k_diag_made"), sem("kd_hi_made"), sem("kd_lo_made")
        scores_full, scores_read = pair("scores_full"), pair("scores_read")
        exps_made, inv_made, probs_made = pair("exps_made"), pair("inv_made"), pair("probs_made")
        pt_full, pt_read = pair("pt_full"), pair("pt_read")
        o_full, o_read = pair("o_full"), pair("o_read")
        passed = {e: sem(f"passed_{e}") for e in ("sp", "pool", "dve")}

        stages = [t[:].rearrange("p a b -> p (a b)")[:, n * STAGE:(n + 1) * STAGE]
                  for t in (kT[2], v[2]) for n in range(2)]
        loads = [(w, slice(c * STAGE, (c + 1) * STAGE)) for w in range(2) for c in range(KV_COLS // STAGE)]
        K1_LOADS, V1_LOADS = range(0, 2), range(2, 4)
        WIDE2_LOADS = range(4, 8)

        def fills(j, name):
            return len(FILL_ORDER) * j + FILL_ORDER.index(name) + 1

        def o_uses(j, l, what):
            return len(O_USES) * j + O_USES.index((l, what)) + 1

        def q_uses(j, l, b, part):
            return len(Q_USES) * j + Q_USES.index((l, b, part)) + 1

        def narrow_uses(j, l, b):
            return 2 * STREAMS * j + STREAMS * NARROW.index(l) + b + 1

        block = ctx.enter_context(nc.Block())

        @block.sync
        def _(sp):
            sp.dma_start(c_in[:], ctxT[:, :, 0:TOK]).then_inc(c_loaded, 16)
            sp.dma_start(x_in[:], xT[:, 0:TOK].rearrange("c (b t) -> c b t", b=STREAMS)).then_inc(x_loaded, 16)
            sp.dma_start(wn[:], narrow_w).then_inc(narrow_loaded, 16)
            sp.dma_start(consts[:], constants).then_inc(setup_loaded, 16)
            sp.dma_start(vec[:], vectors).then_inc(setup_loaded, 16)
            sp.dma_start(mask[:], masks).then_inc(setup_loaded, 16)
            sp.dma_start(tok_i[:], tokens.broadcast_to([P, 8])).then_inc(setup_loaded, 16)
            for n, (w, cols) in enumerate(loads):
                if n >= STAGES:
                    sp.wait_ge(stage_lo, n - STAGES + 1)
                sp.dma_start(stages[n % STAGES], kv_w[:, w, cols]).then_inc(stage_loaded[n % STAGES], 16)
                if n == 3:
                    sp.dma_start(w_qo[:], qo_w).then_inc(qo_loaded, 16)

            def load_context(j):
                sp.wait_ge(c_split, j)
                sp.wait_ge(fill_full, fills(j - 1, "vn"))
                sp.sem_inc(passed["sp"], 1)
                sp.dma_start(c_in[:], ctxT[:, :, bass.ds(j * TOK, TOK)]).then_inc(c_loaded, 16)

            def load_x(j):
                for b in range(STREAMS):
                    sp.wait_ge(o_read[b], FREE + o_uses(j - 1, 0, "o"))
                    sp.sem_inc(passed["sp"], 1)
                sp.dma_start(x_in[:], xT[:, bass.ds(j * TOK, TOK)].rearrange("c (b t) -> c b t", b=STREAMS)
                             ).then_inc(x_loaded, 16)

            def store(i):
                for b in range(STREAMS):
                    sp.wait_ge(o_read[b], FREE + o_uses(i, 3, "o"))
                    sp.sem_inc(passed["sp"], 1)
                    sp.dma_start(outT[:, bass.ds(i * TOK + b * T, T)], x_out[:, b, :]).then_inc(out_stored[b], 16)

            with sp.Fori(0, TURNS - 1) as i:
                load_context(i + 1)
                load_x(i + 1)
                store(i)
            store(TURNS - 1)
            for b in range(STREAMS):
                sp.wait_ge(out_stored[b], 16 + 16 * TURNS)

        @block.gpsimd
        def _(pool):
            nc.gpsimd.memset(half_power[:], -0.5)
            nc.gpsimd.memset(mean_w[:], 1.0 / C).then_inc(ones_made, 1)
            nc.gpsimd.iota(key_i[:], pattern=[[1, S]], base=0, channel_multiplier=0).then_inc(keys_made, 1)

            def split_context(j):
                pool.wait_ge(c_loaded, 16 * j + 16)
                pool.sem_inc(passed["pool"], 1)
                nc.gpsimd.tensor_copy(c_hi[:], c_in[:]).then_inc(c_rounded, 1)
                pool.wait_ge(c_rounded, j + 1)
                nc.gpsimd.tensor_tensor(c_lo[:], c_in[:], c_hi[:].bitcast(F32), ALU.subtract).then_inc(c_split, 1)

            def diagonal_keys(j, l):
                n = NARROW.index(l)
                pool.wait_ge(fill_read, FREE + fills(j, "kn"))
                keys = k_narrow[:, n, :].rearrange("p (b k) -> p b k", b=STREAMS)
                for b in range(STREAMS):
                    last = nc.gpsimd.tensor_tensor(
                        k_diag[:, b], keys[:, b].unsqueeze(1).broadcast_to([P, REP, S]),
                        rep_mask.unsqueeze(2).broadcast_to([P, REP, S]), ALU.mult)
                last.then_inc(k_diag_made, 1)

            def diagonal_rest(j, l):
                pool.wait_ge(kd_hi_made, 2 * j + NARROW.index(l) + 1)
                nc.gpsimd.tensor_tensor(kd_lo[l][:], k_diag[:], kd_hi[l][:].bitcast(F32),
                                        ALU.subtract).then_inc(kd_lo_made, 1)

            def inverse_root(j, l, b):
                pool.wait_ge(rms_out, narrow_uses(j, l, b))
                nc.gpsimd.tensor_tensor(inv_rms[:, b:b + 1], rms[:, b:b + 1], half_power[:],
                                        ALU.pow).then_inc(rms_made, 1)

            def normalise(j, l, b, h):
                n = octet(l, b, h)
                for side in range(2):
                    pool.wait_ge(inv_made[side], OCTETS * j + n + 1)
                    p4 = probs[:, n % 2, side, :].rearrange("p (h k) -> p h k", h=4)
                    nc.gpsimd.tensor_tensor(
                        p4, p4, inv[:, n % 2, side, :].unsqueeze(2).broadcast_to([P, 4, S]), ALU.mult,
                    ).then_inc(probs_made[side], 1)

            def front(j, l, b, phase):
                if phase == 0 and l in NARROW:
                    inverse_root(j, l, b)
                if phase == 2:
                    normalise(j, l, b, 0)

            def turn(i, last):
                for slot, phase, fb, front_at, bb, back_at, _ in slot_work(i, last):
                    if phase == 0:
                        normalise(*back_at, bb, 1)
                    if front_at:
                        front(*front_at, fb, phase)
                    if slot == KEYS3_SLOT:
                        diagonal_keys(i, 3)
                    if slot == KEYS3_SLOT + 3:
                        diagonal_rest(i, 3)
                    if not last and slot == SPLIT_SLOT:
                        pool.wait_ge(fill_full, fills(i, "v2.3"))
                        split_context(i + 1)
                    if not last and slot == KEYS0_SLOT:
                        diagonal_keys(i + 1, 0)
                    if not last and slot == KEYS0_SLOT + 3:
                        diagonal_rest(i + 1, 0)

            split_context(0)
            pool.wait_ge(setup_loaded, 16 * 4)
            diagonal_keys(0, 0)
            diagonal_rest(0, 0)
            for phase in range(3):
                front(0, 0, 0, phase)
            with pool.Fori(0, TURNS - 1) as i:
                turn(i, False)
            turn(TURNS - 1, True)

        @block.scalar
        def _(act):
            def round_weights(which):
                for n in which:
                    w, cols = loads[n]
                    act.wait_ge(stage_loaded[n % STAGES], 16 * (n // STAGES + 1))
                    nc.scalar.activation(w_hi[:, w, cols], stages[n % STAGES], ACT.Copy).then_inc(stage_hi, 1)

            def fill_out(j, name):
                if name == "kn":
                    dst = k_narrow[:].rearrange("p l t -> p (l t)")
                elif name == "vn":
                    dst = v_narrow[:].rearrange("p b l n -> p (b l n)")
                elif name[0] == "k":
                    l, n = int(name[1]), int(name[3])
                    dst = kT[l][:, 2 * n:2 * n + 2, :].rearrange("p c t -> p (c t)")
                else:
                    l, n = int(name[1]), int(name[3])
                    dst = v[l][:, n // 2, n % 2 * BANK:(n % 2 + 1) * BANK]
                act.wait_ge(fill_full, fills(j, name))
                nc.scalar.activation(dst, fill_ps[:], ACT.Copy).then_inc(fill_read, 1)

            def diagonal_keys(j, l):
                act.wait_ge(k_diag_made, 2 * j + NARROW.index(l) + 1)
                nc.scalar.activation(kd_hi[l][:].rearrange("p b r k -> p (b r k)"),
                                     k_diag[:].rearrange("p b r k -> p (b r k)"), ACT.Copy).then_inc(kd_hi_made, 1)

            def exponentials(j, l, b, h):
                n = octet(l, b, h)
                for side in range(2):
                    act.wait_ge(scores_read[side], FREE + OCTETS * j + n + 1)
                    for q in range(4):
                        e = probs[:, n % 2, side, q * S:(q + 1) * S]
                        last = nc.scalar.activation(e, e, ACT.Exp, scale=-1.0, bias=negmax[:, n % 2, side, q:q + 1],
                                                    accum_out=rowsum[:, n % 2, side, q:q + 1])
                    last.then_inc(exps_made[side], 1)

            def turn(i, last):
                for slot, phase, fb, front_at, bb, back_at, fill in slot_work(i, last):
                    if front_at and phase > 0:
                        exponentials(*front_at, fb, phase - 1)
                    for j, name in fill:
                        fill_out(j, name)
                    if slot == KEYS3_SLOT + 2:
                        diagonal_keys(i, 3)
                    if not last and slot == KEYS0_SLOT + 2:
                        diagonal_keys(i + 1, 0)

            fill_out(0, "kn")
            round_weights(K1_LOADS)
            diagonal_keys(0, 0)
            round_weights(V1_LOADS)
            act.wait_ge(setup_done, 1)
            exponentials(0, 0, 0, 0)
            exponentials(0, 0, 0, 1)
            for name in EARLY[1:]:
                fill_out(0, name)
            round_weights(WIDE2_LOADS)
            act.wait_ge(stage_lo, len(loads))
            with act.Fori(0, TURNS - 1) as i:
                turn(i, False)
            turn(TURNS - 1, True)

        @block.vector
        def _(dve):
            steps = [0]

            def setup(ins):
                steps[0] += 1
                ins.then_inc(setup_step, 1)
                dve.wait_ge(setup_step, steps[0])

            def norm_weights():
                for n in range(2):
                    wq = wn[:, NQ + n * C:NQ + (n + 1) * C]
                    setup(nc.vector.tensor_scalar(wq, wq, vec[:, n:n + 1], None, ALU.mult))

            def column_bias():
                setup(nc.vector.tensor_copy(key_f[:], key_i[:]))
                setup(nc.vector.tensor_copy(tok_f[:, 0:8], tok_i[:]))
                setup(nc.vector.tensor_scalar(tok_f[:, 8:16], tok_f[:, 0:8], float(S), None, ALU.add))
                setup(nc.vector.tensor_scalar(suppress[:], mask[:], -SUPPRESS, SUPPRESS, ALU.mult, ALU.add))
                for l in range(2):
                    for m in range(2):
                        first = 4 * l + 2 * m
                        setup(nc.vector.tensor_scalar(hit[:, m, :], key_f[:], tok_f[:, first:first + 1], None,
                                                      ALU.is_equal))
                        for t in (first + 1, first + 8, first + 9):
                            setup(nc.vector.scalar_tensor_tensor(
                                out=hit[:, m, :], in0=key_f[:], scalar=tok_f[:, t:t + 1], in1=hit[:, m, :],
                                op0=ALU.is_equal, op1=ALU.max))
                    setup(nc.vector.tensor_scalar(col_bias[:, l, :], hit[:, 1, :], -1.0, 1.0, ALU.mult, ALU.add))
                    setup(nc.vector.tensor_tensor(hit[:, 0, :], hit[:, 0, :], col_bias[:, l, :], ALU.mult))
                    setup(nc.vector.tensor_scalar(hit[:, 1, :], hit[:, 1, :], suppress[:, 1:2], None, ALU.mult))
                    setup(nc.vector.scalar_tensor_tensor(
                        out=col_bias[:, l, :], in0=hit[:, 0, :], scalar=suppress[:, 0:1], in1=hit[:, 1, :],
                        op0=ALU.mult, op1=ALU.add))

            def split_weights(which):
                for n in which:
                    w, cols = loads[n]
                    dve.wait_ge(stage_hi, n + 1)
                    nc.vector.tensor_tensor(w_lo[:, w, cols], stages[n % STAGES], w_hi[:, w, cols].bitcast(F32),
                                            ALU.subtract).then_inc(stage_lo, 1)

            def square(b, src):
                nc.vector.tensor_tensor(x_sq[:, b, :], src, src, ALU.mult).then_inc(sq_ready, 1)

            def narrow_queries(j, l, b):
                use = narrow_uses(j, l, b)
                dve.wait_ge(q_full, q_uses(j, l, b, 0))
                nc.vector.tensor_scalar(rms[:, b:b + 1], q_ps[:, T:T + 1], EPS, None, ALU.add).then_inc(rms_out, 1)
                nc.vector.tensor_tensor(
                    q_group[:], q_ps[:, 0:T].unsqueeze(1).broadcast_to([P, KV_HEADS, T]),
                    group_mask.unsqueeze(2).broadcast_to([P, KV_HEADS, T]), ALU.mult).then_inc(qg_made, 1)
                dve.wait_ge(qg_made, use)
                dve.sem_inc(q_read, 1)
                nc.vector.tensor_copy(qg_hi[:], q_group[:]).then_inc(qg_hi_made, 1)
                dve.wait_ge(qg_hi_made, use)
                nc.vector.tensor_tensor(qg_lo[:], q_group[:], qg_hi[:].bitcast(F32),
                                        ALU.subtract).then_inc(qg_lo_made, 1)

            def wide_queries(j, l, b, part):
                dve.wait_ge(q_full, q_uses(j, l, b, part))
                nc.vector.tensor_scalar(qT[:, 4 * part:4 * part + 4, b, :],
                                        q_ps[:].rearrange("p (c t) -> p c t", c=4), -WIDE_D ** -0.5, None,
                                        ALU.mult).then_inc(q_read, 1)

            def scores_out(j, l, b, h, side):
                n = octet(l, b, h)
                bias = col_bias[:, 2 if l in NARROW else l - 1, :]
                scale = inv_rms[:, b:b + 1] if l in NARROW else 1.0
                if l in NARROW and h == 0 and side == 0:
                    dve.wait_ge(rms_made, narrow_uses(j, l, b))
                    dve.sem_inc(passed["dve"], 1)
                dve.wait_ge(scores_full[side], OCTETS * j + n + 1)
                dve.sem_inc(passed["dve"], 1)
                for q in range(4):
                    cols = slice(q * S, (q + 1) * S)
                    last = nc.vector.tensor_tensor_reduce(
                        out=probs[:, n % 2, side, cols], in0=scores_ps[side][:, cols], in1=bias, scale=scale,
                        scalar=HUGE, op0=ALU.add, op1=ALU.min, accum_out=negmax[:, n % 2, side, q:q + 1])
                last.then_inc(scores_read[side], 1)

            def inverse_sums(j, l, b, h, side):
                n = octet(l, b, h)
                dve.wait_ge(exps_made[side], OCTETS * j + n + 1)
                nc.vector.reciprocal(inv[:, n % 2, side, :], rowsum[:, n % 2, side, :]).then_inc(inv_made[side], 1)

            def transposes_out(j, l, b, h, side):
                n = octet(l, b, h)
                dve.wait_ge(pt_full[side], OCTETS * j + n + 1)
                nc.vector.tensor_copy(probsT[:, side, :], pt_ps[side][:]).then_inc(pt_read[side], 1)

            def outputs_out(j, l, b, h):
                if l in NARROW:
                    dve.wait_ge(o_full[b], o_uses(j, l, "pv"))
                    nc.vector.tensor_copy(oT[:, 0:REP, b, :],
                                          o_ps[b][:].rearrange("p (r q) -> p r q", r=REP)).then_inc(o_read[b], 1)
                else:
                    dve.wait_ge(o_full[b], o_uses(j, l, f"pv{h}"))
                    nc.vector.tensor_copy(oT[:, 4 * h:4 * h + 4, b, :],
                                          o_ps[b][:].rearrange("p (c q) -> p c q", c=4)).then_inc(o_read[b], 1)

            def add_input(j, l, b):
                if l == 3:
                    dve.wait_ge(out_stored[b], 16 * j + 16)
                    dve.sem_inc(passed["dve"], 1)
                dve.wait_ge(o_full[b], o_uses(j, l, "o"))
                y = o_ps[b][:, 0:T]
                if l == 0:
                    ins = nc.vector.tensor_tensor(x[:, b, :], y, x_in[:, b, :], ALU.add)
                elif l < 3:
                    ins = nc.vector.scalar_tensor_tensor(out=x[:, b, :], in0=y, scalar=vec[:, l + 1:l + 2],
                                                         in1=x[:, b, :], op0=ALU.add, op1=ALU.add)
                else:
                    ins = nc.vector.tensor_tensor(x_out[:, b, :], y, x[:, b, :], ALU.add)
                ins.then_inc(o_read[b], 1)
                if l == 2:
                    dve.wait_ge(o_read[b], FREE + o_uses(j, l, "o"))
                    square(b, x[:, b, :])

            def input_squares(j, l, b):
                if l == 0:
                    dve.wait_ge(x_loaded, 16 * j + 16)
                    square(b, x_in[:, b, :])

            def front_queries(j, l, b, part):
                if l in NARROW and part == 0:
                    narrow_queries(j, l, b)
                if l not in NARROW:
                    wide_queries(j, l, b, part)

            def turn(i, last):
                for slot, phase, fb, front_at, bb, back_at, _ in slot_work(i, last):
                    j, l = back_at
                    if phase == 0:
                        if front_at:
                            input_squares(*front_at, fb)
                        inverse_sums(j, l, bb, 1, 0)
                        transposes_out(j, l, bb, 0, 0)
                        transposes_out(j, l, bb, 0, 1)
                        inverse_sums(j, l, bb, 1, 1)
                        if front_at:
                            front_queries(*front_at, fb, 0)
                        if l not in NARROW:
                            outputs_out(j, l, bb, 0)
                        if front_at:
                            front_queries(*front_at, fb, 1)
                    if phase == 1:
                        for side in range(2):
                            transposes_out(j, l, bb, 1, side)
                        if front_at:
                            for side in range(2):
                                scores_out(*front_at, fb, 0, side)
                        outputs_out(j, l, bb, 1)
                    if phase == 2:
                        if front_at:
                            for side in range(2):
                                inverse_sums(*front_at, fb, 0, side)
                                scores_out(*front_at, fb, 1, side)
                        add_input(j, l, bb)

            for s in (fill_read, q_read, *scores_read, *pt_read, *o_read):
                dve.sem_inc(s, FREE)
            for s in out_stored:
                dve.sem_inc(s, 16)
            nc.vector.memset(col_bias[:, 2, :], 0.0)
            dve.wait_ge(setup_loaded, 16 * 4)
            dve.wait_ge(narrow_loaded, 16)
            norm_weights()
            nc.vector.memset(rowsum[:, 0, 0, 0:1], 0.0).then_inc(setup_done, 1)
            input_squares(0, 0, 0)
            front_queries(0, 0, 0, 0)
            split_weights(K1_LOADS)
            for side in range(2):
                scores_out(0, 0, 0, 0, side)
            for side in range(2):
                inverse_sums(0, 0, 0, 0, side)
                scores_out(0, 0, 0, 1, side)
            split_weights(V1_LOADS)
            dve.wait_ge(keys_made, 1)
            column_bias()
            split_weights(WIDE2_LOADS)
            with dve.Fori(0, TURNS - 1) as i:
                turn(i, False)
            turn(TURNS - 1, True)

        @block.tensor
        def _(pe):
            def three(out, stationary, moving):
                for n, ((a_hi, a_lo), (b_hi, b_lo)) in enumerate(zip(stationary, moving)):
                    nc.tensor.matmul(out, a_hi, b_hi, start=(n == 0), stop=False)
                    nc.tensor.matmul(out, a_lo, b_hi, start=False, stop=False)
                    last = nc.tensor.matmul(out, a_hi, b_lo, start=False, stop=(n == len(moving) - 1))
                return last

            def both(first, w, cols):
                return w_hi[:, w, first:first + cols], w_lo[:, w, first:first + cols]

            def project_context(j, name):
                pe.wait_ge(fill_read, FREE + fills(j, name) - 1)
                if name == "kn":
                    pe.wait_ge(c_loaded, 16 * j + 16)
                    for n in range(2):
                        for c in range(CC):
                            first = NK + (n * CC + c) * C
                            last = nc.tensor.matmul(fill_ps[:, n * TOK:(n + 1) * TOK], wn[:, first:first + C],
                                                    c_in[:, c, :], start=(c == 0), stop=(c == CC - 1))
                elif name == "vn":
                    for b in range(STREAMS):
                        for c in range(CC):
                            first = NV + c * 2 * C
                            last = nc.tensor.matmul(fill_ps[:, b * 2 * C:(b + 1) * 2 * C],
                                                    c_in[:, c, b * S:(b + 1) * S], wn[:, first:first + 2 * C],
                                                    start=(c == 0), stop=(c == CC - 1))
                else:
                    pe.wait_ge(c_split, j + 1)
                    l, m = int(name[1]), int(name[3])
                    if name[0] == "k":
                        for n in range(2):
                            chunk = 2 * m + n
                            last = three(fill_ps[:, n * TOK:(n + 1) * TOK],
                                         [both(WK + c * INNER + chunk * P, l - 1, P) for c in range(CC)],
                                         [(c_hi[:, c, :], c_lo[:, c, :]) for c in range(CC)])
                    else:
                        b, n = m // 2, m % 2
                        keys = slice(b * S, (b + 1) * S)
                        last = three(fill_ps[:], [(c_hi[:, c, keys], c_lo[:, c, keys]) for c in range(CC)],
                                     [both(WV + c * INNER + n * BANK, l - 1, BANK) for c in range(CC)])
                last.then_inc(fill_full, 1)

            def queries(j, l, b, part):
                if l in NARROW and part == 1:
                    return
                use = q_uses(j, l, b, part)
                pe.wait_ge(q_read, FREE + use - 1)
                if l in NARROW:
                    pe.wait_ge(sq_ready, narrow_uses(j, l, b))
                    first = NQ + NARROW.index(l) * C
                    src = (x_in if l == 0 else x)[:, b, :]
                    nc.tensor.matmul(q_ps[:, 0:T], wn[:, first:first + C], src, start=True, stop=True)
                    nc.tensor.matmul(q_ps[:, T:2 * T], x_sq[:, b, :], mean_w[:], start=True,
                                     stop=True).then_inc(q_full, 1)
                    return
                if part == 0:
                    pe.wait_ge(o_read[b], FREE + o_uses(j, l - 1, "o"))
                for n in range(4):
                    first = WQ + (4 * part + n) * P
                    last = nc.tensor.matmul(q_ps[:, n * T:(n + 1) * T], w_qo[:, l - 1, first:first + P], x[:, b, :],
                                            start=True, stop=True)
                last.then_inc(q_full, 1)

            def scores(j, l, b, h):
                n = octet(l, b, h)
                pe.wait_ge(scores_read[0], FREE + OCTETS * j + n)
                if l in NARROW:
                    pe.wait_ge(kd_lo_made, 2 * j + NARROW.index(l) + 1)
                    pe.wait_ge(qg_lo_made, narrow_uses(j, l, b))
                    for side in range(2):
                        g = 2 * h + side
                        if side == 1:
                            pe.wait_ge(scores_read[1], FREE + OCTETS * j + n)
                        three(scores_ps[side][:], [(qg_hi[:, g, :], qg_lo[:, g, :])],
                              [(kd_hi[l][:, b].rearrange("p r k -> p (r k)"),
                                kd_lo[l][:, b].rearrange("p r k -> p (r k)"))]).then_inc(scores_full[side], 1)
                    return
                if h == 0:
                    pe.wait_ge(fill_read, FREE + fills(j, f"k{l}.3"))
                pe.wait_ge(q_read, FREE + q_uses(j, l, b, h))
                for side in range(2):
                    rows = slice(side * WIDE_D, (side + 1) * WIDE_D)
                    if side == 1:
                        pe.wait_ge(scores_read[1], FREE + OCTETS * j + n)
                    for c in range(4):
                        last = nc.tensor.matmul(scores_ps[side][:, c * S:(c + 1) * S], qT[rows, 4 * h + c, b, :],
                                                kT[l][rows, 4 * h + c, b * S:(b + 1) * S], start=True, stop=True)
                    last.then_inc(scores_full[side], 1)

            def transpose_probs(j, l, b, h):
                n = octet(l, b, h)
                for side in range(2):
                    pe.wait_ge(probs_made[side], OCTETS * j + n + 1)
                    pe.wait_ge(pt_read[side], FREE + OCTETS * j + n)
                    for q in range(4):
                        cols = slice(q * S, (q + 1) * S)
                        last = nc.tensor.transpose(pt_ps[side][:, cols], probs[:, n % 2, side, cols], identity)
                    last.then_inc(pt_full[side], 1)

            def weighted_values(j, l, b, h):
                n = octet(l, b, h)
                if l in NARROW:
                    if h == 0:
                        pe.wait_ge(o_read[b], FREE + o_uses(j, l, "pv") - 1)
                        pe.wait_ge(fill_read, FREE + fills(j, "vn"))
                    for side in range(2):
                        g = 2 * h + side
                        pe.wait_ge(pt_read[side], FREE + OCTETS * j + n + 1)
                        last = nc.tensor.matmul(o_ps[b][32 * g:32 * g + 32, :],
                                                v_narrow[:, b, NARROW.index(l), 32 * g:32 * g + 32],
                                                probsT[:, side, :], start=True, stop=True)
                    if h == 1:
                        last.then_inc(o_full[b], 1)
                    return
                pe.wait_ge(o_read[b], FREE + o_uses(j, l, f"pv{h}") - 1)
                if h == 0:
                    pe.wait_ge(fill_read, FREE + fills(j, f"v{l}.3"))
                for side in range(2):
                    pe.wait_ge(pt_read[side], FREE + OCTETS * j + n + 1)
                for c in range(4):
                    for side in range(2):
                        head = 8 * h + 2 * c + side
                        last = nc.tensor.matmul(
                            o_ps[b][side * WIDE_D:(side + 1) * WIDE_D, c * T:(c + 1) * T],
                            v[l][:, b, head * WIDE_D:(head + 1) * WIDE_D], probsT[:, side, c * T:(c + 1) * T],
                            start=True, stop=True)
                last.then_inc(o_full[b], 1)

            def output_projection(j, l, b):
                pe.wait_ge(o_read[b], FREE + o_uses(j, l, "o") - 1)
                for c in range(REP if l in NARROW else IC):
                    if l in NARROW:
                        first = NO + (NARROW.index(l) * REP + c) * C
                        w = wn[:, first:first + C]
                    else:
                        first = WO + c * C
                        w = w_qo[:, l - 1, first:first + C]
                    last = nc.tensor.matmul(o_ps[b][:, 0:T], w, oT[:, c, b, :], start=(c == 0),
                                            stop=(c == (REP if l in NARROW else IC) - 1))
                last.then_inc(o_full[b], 1)

            def turn(i, last):
                for slot, phase, fb, front_at, bb, back_at, fill in slot_work(i, last):
                    if phase == 0:
                        transpose_probs(*back_at, bb, 0)
                        if front_at:
                            queries(*front_at, fb, 0)
                        weighted_values(*back_at, bb, 0)
                        if front_at:
                            queries(*front_at, fb, 1)
                    if phase == 1:
                        transpose_probs(*back_at, bb, 1)
                        if front_at:
                            scores(*front_at, fb, 0)
                        weighted_values(*back_at, bb, 1)
                    if phase == 2:
                        if front_at:
                            scores(*front_at, fb, 1)
                        output_projection(*back_at, bb)
                    for j, name in fill:
                        project_context(j, name)

            pe.wait_ge(narrow_loaded, 16)
            pe.wait_ge(c_loaded, 16)
            project_context(0, "kn")
            pe.wait_ge(setup_loaded, 16 * 4)
            pe.wait_ge(setup_done, 1)
            pe.wait_ge(ones_made, 1)
            queries(0, 0, 0, 0)
            scores(0, 0, 0, 0)
            scores(0, 0, 0, 1)
            pe.wait_ge(stage_lo, 2)
            for name in EARLY[1:]:
                if name == "v1.0":
                    pe.wait_ge(stage_lo, 4)
                project_context(0, name)
            pe.wait_ge(stage_lo, len(loads))
            pe.wait_ge(qo_loaded, 16)
            with pe.Fori(0, TURNS - 1) as i:
                turn(i, False)
            turn(TURNS - 1, True)


def kernel(**inputs):
    from concourse import bacc
    from concourse.bass_utils import run_bass_kernel_spmd

    a = {k: np.ascontiguousarray(x) for k, x in inputs.items()}

    def chunks(w):
        return w.reshape(-1, P, w.shape[1]).transpose(1, 0, 2).reshape(P, -1)

    def narrow_keys(w):
        w = np.repeat(w.reshape(CT, KV_HEADS, 1, NARROW_D), REP, axis=2)
        return chunks(w.reshape(CT, P))

    def narrow_values(w):
        out = np.zeros((CT, KV_HEADS, 32), w.dtype)
        out[:, :, :NARROW_D] = w.reshape(CT, KV_HEADS, NARROW_D)
        return out.reshape(CC, P, 1, P)

    def narrow_out(w):
        out = np.zeros((KV_HEADS, 32, REP, C), w.dtype)
        out[:, :NARROW_D] = w.reshape(KV_HEADS, REP, NARROW_D, C).transpose(0, 2, 1, 3)
        return out.reshape(P, REP * C)

    narrow_v = np.concatenate([narrow_values(a[f"L{l}_xattn_wv"]) for l in NARROW], axis=2)
    narrow_w = np.concatenate(
        [a[f"L{l}_xattn_wq"] for l in NARROW] + [narrow_keys(a[f"L{l}_xattn_wk"]) for l in NARROW]
        + [narrow_v.transpose(1, 0, 2, 3).reshape(P, -1)] + [narrow_out(a[f"L{l}_xattn_wo"]) for l in NARROW], axis=1)
    kv_w, qo_w = (np.stack([np.concatenate([chunks(a[f"L{l}_xattn_{w}"]) for w in names], axis=1) for l in (1, 2)],
                           axis=1) for names in (("Wk", "Wv"), ("Wq", "Wo")))
    vectors = np.stack([a["L0_xattn_norm_w"], a["L3_xattn_norm_w"], a["L1_xattn_bo"], a["L2_xattn_bo"]], axis=1)
    masks = np.stack([a["mask_S_fk1"], a["mask_S_fk0"]], axis=1)
    tokens = np.concatenate([a[f"L{l}_xattn_token_indices_{m}"] for l in (1, 2) for m in "AB"])[None, :]
    if tokens.dtype.itemsize == 8:
        tokens = tokens.view(np.int32)[:, ::2]
    row = np.arange(P)
    constants = np.concatenate([np.eye(P), row[:, None] // NARROW_D % REP == np.arange(REP),
                                (row[:, None] // (NARROW_D * REP) == np.arange(KV_HEADS))
                                * -(1.0 / np.sqrt(np.float32(NARROW_D)))], axis=1)
    arrays = {
        "xT": a["x"].reshape(B * T, C).T,
        "ctxT": a["ctx_2048"].reshape(B * S, CC, P).transpose(2, 1, 0),
        "narrow_w": narrow_w, "kv_w": kv_w, "qo_w": qo_w, "vectors": vectors, "masks": masks, "tokens": tokens,
        "constants": constants.astype(np.float32),
    }
    nc = bacc.Bacc("TRN2", target_bir_lowering=False, num_devices=1)
    arrays = {f"in_{k}": np.ascontiguousarray(x) for k, x in arrays.items()}
    args = [nc.dram_tensor(k, x.shape, mybir.dt.from_np(x.dtype), kind="ExternalInput").ap()
            for k, x in arrays.items()]
    args.append(nc.dram_tensor("outT", (C, B * T), F32, kind="ExternalOutput").ap())
    build(nc, *args)
    r = run_bass_kernel_spmd(nc, [arrays], core_ids=[0])
    return np.ascontiguousarray(r.results[0]["outT"].T).reshape(B, T, C)
```

```python
from contextlib import ExitStack

import numpy as np

import concourse.bass as bass
from concourse import mybir

ALU = mybir.AluOpType
ACT = mybir.ActivationFunctionType
F32 = mybir.dt.float32
F32R = mybir.dt.float32r
I32 = mybir.dt.int32

P = 128
B, T, C = 8, 128, 128
S, CT = 128, 256
HEADS = 16
WIDE_D, NARROW_D = 64, 8
KV_HEADS = 4
REP = HEADS // KV_HEADS
INNER = HEADS * WIDE_D
SUPPRESS = 20.0
EPS = 1e-5
STREAMS = 2
TURNS = B // STREAMS
TOK = STREAMS * T
CC = CT // P
IC = INNER // P
BANK = 512
LAYERS = 4
NARROW = (0, 3)
OCTETS = LAYERS * STREAMS * 2
LAYER_MASKS = 2 * 2
HUGE = 3.0e38
FREE = 1

KV_C = KV_HEADS * NARROW_D
NQ, NK = 0, 2 * C
NV = NK + 2 * CC * C
NO = NV + 2 * CC * KV_C
NARROW_COLS = NO + 2 * C
WK, WV = 0, CC * INNER
KV_COLS = 2 * CC * INNER
WQ, WO = 0, INNER
QO_COLS = INNER + IC * C
STAGE = 1024
STAGES = 4

SLOTS = 6
LAG = 3
TURN_SLOTS = SLOTS * LAYERS
FILL = {
    3: ["k2.0"], 4: ["k2.1"], 5: ["k2.2"], 6: ["k2.3"], 7: ["v2.0"], 8: ["v2.1"], 10: ["v2.2"], 12: ["v2.3"],
    15: ["+kn"], 18: ["+k1.0"], 19: ["+k1.1"], 20: ["+k1.2"], 21: ["+k1.3"], 22: ["+v1.0"], 23: ["+v1.1"],
    24: ["+v1.2"], 25: ["+v1.3"], 26: ["+vn"],
}
LOOP_FILL = [name for slot in sorted(FILL) for name in FILL[slot]]
EARLY = [name[1:] for name in LOOP_FILL if name[0] == "+"]
FILL_ORDER = EARLY + [name for name in LOOP_FILL if name[0] != "+"]
SPLIT_SLOT = 14
KEYS3_SLOT, KEYS0_SLOT = 4, 16


def octet(l, b, h):
    return 4 * l + 2 * b + h


O_USES = [(l, what) for l in range(LAYERS) for what in (("pv", "o") if l in NARROW else ("pv0", "pv1", "o"))]
Q_USES = [(l, b, part) for l in range(LAYERS) for b in range(STREAMS) for part in ((0,) if l in NARROW else (0, 1))]


def slot_work(i, last):
    for slot in range(LAG, TURN_SLOTS + LAG):
        front = slot % SLOTS // 3
        back = 1 - front
        n = slot - LAG * front
        front_at = (i, n // SLOTS) if n < TURN_SLOTS else None if last else (i + 1, 0)
        back_at = (i, (slot - LAG * back) // SLOTS)
        fill = [(i + 1, name[1:]) if name[0] == "+" else (i, name) for name in FILL.get(slot, [])
                if not (last and name[0] == "+")]
        yield slot, slot % 3, front, front_at, back, back_at, fill


def build(nc, xT, ctxT, narrow_w, kv_w, qo_w, small, tokens, outT):
    with ExitStack() as ctx:
        def sb(name, shape, dt=F32):
            return ctx.enter_context(nc.sbuf_tensor(name, shape, dt))

        def sem(name):
            return ctx.enter_context(nc.semaphore(name))

        def pair(name):
            return [sem(f"{name}_{i}") for i in range(2)]

        def bank(name):
            return ctx.enter_context(nc.psum_tensor(name, [P, BANK], F32))

        scores_ps = [bank(f"scores_ps{i}") for i in range(2)]
        pt_ps = [bank(f"pt_ps{i}") for i in range(2)]
        o_ps = [bank(f"o_ps{i}") for i in range(2)]
        q_ps, fill_ps = bank("q_ps"), bank("fill_ps")

        wn = sb("wn", [P, NARROW_COLS])
        w_qo = sb("w_qo", [P, 2, QO_COLS])
        w_hi = sb("w_hi", [P, 2, KV_COLS], F32R)
        w_lo = sb("w_lo", [P, 2, KV_COLS], F32R)
        smalls = sb("smalls", [P, P + REP + KV_HEADS + 4 + 2])
        identity = smalls[:, 0:P]
        rep_mask = smalls[:, P:P + REP]
        group_mask = smalls[:, P + REP:P + REP + KV_HEADS]
        vec = smalls[:, P + REP + KV_HEADS:P + REP + KV_HEADS + 4]
        mask = smalls[:, P + REP + KV_HEADS + 4:]
        tok_i = sb("tok_i", [P, LAYER_MASKS, 2], I32)
        tok_f = sb("tok_f", [P, LAYER_MASKS, 4])
        key_i = sb("key_i", [P, S], I32)
        key_f = sb("key_f", [P, S])
        suppress = sb("suppress", [P, 2])
        hits = sb("hits", [P, LAYER_MASKS, S])
        free = sb("free", [P, 2, S])
        col_bias = sb("col_bias", [P, 3, S])
        mean_w = sb("mean_w", [P, P])
        half_power = sb("half_power", [P, 1])

        x_in = sb("x_in", [P, STREAMS, T])
        x = sb("x", [P, STREAMS, T])
        x_out = sb("x_out", [P, STREAMS, T])
        x_sq = sb("x_sq", [P, STREAMS, T])
        rms = sb("rms", [P, STREAMS])
        inv_rms = sb("inv_rms", [P, STREAMS])
        c_in = sb("c_in", [P, CC, TOK])
        c_hi = sb("c_hi", [P, CC, TOK], F32R)
        c_lo = sb("c_lo", [P, CC, TOK], F32R)
        kT = {l: sb(f"kT{l}", [P, IC, TOK]) for l in (1, 2)}
        v = {l: sb(f"v{l}", [P, STREAMS, INNER]) for l in (1, 2)}
        k_narrow = sb("k_narrow", [P, 2, TOK])
        v_narrow = sb("v_narrow", [P, STREAMS, 2, REP, P])
        k_diag = sb("k_diag", [P, STREAMS, REP, S])
        kd_hi = {l: sb(f"kd_hi{l}", [P, STREAMS, REP, S], F32R) for l in NARROW}
        kd_lo = {l: sb(f"kd_lo{l}", [P, STREAMS, REP, S], F32R) for l in NARROW}
        qT = sb("qT", [P, IC, STREAMS, T])
        q_group = sb("q_group", [P, KV_HEADS, T])
        qg_hi = sb("qg_hi", [P, KV_HEADS, T], F32R)
        qg_lo = sb("qg_lo", [P, KV_HEADS, T], F32R)
        oT = sb("oT", [P, IC, STREAMS, T])
        probs = sb("probs", [P, 2, 2, BANK])
        probsT = sb("probsT", [P, 2, BANK])
        negmax = sb("negmax", [P, 2, 2, 4])
        rowsum = sb("rowsum", [P, 2, 2, 4])
        inv = sb("inv", [P, 2, 2, 4])

        equal = qT[:].rearrange("p c b t -> p (c b t)")[:, 0:LAYER_MASKS * S * 4].rearrange(
            "p (l s t) -> p l s t", l=LAYER_MASKS, t=4)

        tokens_loaded, smalls_loaded, qo_loaded = sem("tokens_loaded"), sem("smalls_loaded"), sem("qo_loaded")
        narrow_qk_loaded, narrow_vo_loaded = sem("narrow_qk_loaded"), sem("narrow_vo_loaded")
        norms_folded = sem("norms_folded")
        stage_loaded = [sem(f"stage_loaded_{i}") for i in range(STAGES)]
        stage_hi, stage_lo = sem("stage_hi"), sem("stage_lo")
        keys_made, ones_made, zeros_made, setup_step = (
            sem("keys_made"), sem("ones_made"), sem("zeros_made"), sem("setup_step"))
        x_loaded, c_loaded, out_stored = sem("x_loaded"), sem("c_loaded"), pair("out_stored")
        c_rounded, c_split = sem("c_rounded"), sem("c_split")
        sq_ready, rms_out, rms_made = sem("sq_ready"), sem("rms_out"), sem("rms_made")
        fill_full, fill_read = sem("fill_full"), sem("fill_read")
        q_full, q_read = sem("q_full"), sem("q_read")
        qg_made, qg_hi_made, qg_lo_made = sem("qg_made"), sem("qg_hi_made"), sem("qg_lo_made")
        k_diag_made, kd_hi_made, kd_lo_made = sem("k_diag_made"), sem("kd_hi_made"), sem("kd_lo_made")
        scores_full, scores_read = pair("scores_full"), pair("scores_read")
        exps_made, inv_made, probs_made = pair("exps_made"), pair("inv_made"), pair("probs_made")
        pt_full, pt_read = pair("pt_full"), pair("pt_read")
        o_full, o_read = pair("o_full"), pair("o_read")
        passed = {e: sem(f"passed_{e}") for e in ("sp", "pool", "dve")}

        stages = [t[:].rearrange("p a b -> p (a b)")[:, n * STAGE:(n + 1) * STAGE]
                  for t in (kT[2], v[2]) for n in range(2)]
        loads = [(w, slice(c * STAGE, (c + 1) * STAGE)) for w in range(2) for c in range(KV_COLS // STAGE)]
        K1_LOADS, V1_LOADS = range(0, 2), range(2, 4)
        WIDE2_LOADS = range(4, 8)

        def fills(j, name):
            return len(FILL_ORDER) * j + FILL_ORDER.index(name) + 1

        def o_uses(j, l, what):
            return len(O_USES) * j + O_USES.index((l, what)) + 1

        def q_uses(j, l, b, part):
            return len(Q_USES) * j + Q_USES.index((l, b, part)) + 1

        def narrow_uses(j, l, b):
            return 2 * STREAMS * j + STREAMS * NARROW.index(l) + b + 1

        def fill_bank(banks, name):
            return o_ps[1] if banks == 2 and EARLY.index(name) % 2 else fill_ps

        block = ctx.enter_context(nc.Block())

        @block.sync
        def _(sp):
            sp.dma_start(tok_i[:].rearrange("p l t -> p (l t)"), tokens.broadcast_to([P, 2 * LAYER_MASKS])
                         ).then_inc(tokens_loaded, 16)
            sp.dma_start(c_in[:], ctxT[:, :, 0:TOK]).then_inc(c_loaded, 16)
            sp.dma_start(wn[:, NQ:NV], narrow_w[:, NQ:NV]).then_inc(narrow_qk_loaded, 16)
            sp.dma_start(x_in[:], xT[:, 0:TOK].rearrange("c (b t) -> c b t", b=STREAMS)).then_inc(x_loaded, 16)
            sp.dma_start(smalls[:], small).then_inc(smalls_loaded, 16)
            for n, (w, cols) in enumerate(loads):
                if n >= STAGES:
                    sp.wait_ge(stage_lo, n - STAGES + 1)
                sp.dma_start(stages[n % STAGES], kv_w[:, w, cols]).then_inc(stage_loaded[n % STAGES], 16)
                if n == STAGES - 1:
                    sp.dma_start(wn[:, NV:], narrow_w[:, NV:]).then_inc(narrow_vo_loaded, 16)
            sp.dma_start(w_qo[:], qo_w).then_inc(qo_loaded, 16)

            def load_context(j):
                sp.wait_ge(c_split, j)
                sp.wait_ge(fill_full, fills(j - 1, "vn"))
                sp.sem_inc(passed["sp"], 1)
                sp.dma_start(c_in[:], ctxT[:, :, bass.ds(j * TOK, TOK)]).then_inc(c_loaded, 16)

            def load_x(j):
                for b in range(STREAMS):
                    sp.wait_ge(o_read[b], FREE + o_uses(j - 1, 0, "o"))
                    sp.sem_inc(passed["sp"], 1)
                sp.dma_start(x_in[:], xT[:, bass.ds(j * TOK, TOK)].rearrange("c (b t) -> c b t", b=STREAMS)
                             ).then_inc(x_loaded, 16)

            def store(i):
                for b in range(STREAMS):
                    sp.wait_ge(o_read[b], FREE + o_uses(i, 3, "o"))
                    sp.sem_inc(passed["sp"], 1)
                    sp.dma_start(outT[:, bass.ds(i * TOK + b * T, T)], x_out[:, b, :]).then_inc(out_stored[b], 16)

            with sp.Fori(0, TURNS - 1) as i:
                load_context(i + 1)
                load_x(i + 1)
                store(i)
            store(TURNS - 1)
            for b in range(STREAMS):
                sp.wait_ge(out_stored[b], 16 + 16 * TURNS)

        @block.gpsimd
        def _(pool):
            nc.gpsimd.memset(half_power[:], -0.5)
            nc.gpsimd.memset(mean_w[:], 1.0 / C).then_inc(ones_made, 1)
            nc.gpsimd.iota(key_i[:], pattern=[[1, S]], base=0, channel_multiplier=0).then_inc(keys_made, 1)

            nc.gpsimd.memset(v_narrow[:], 0.0).then_inc(zeros_made, 1)

            def split_context(j):
                pool.wait_ge(c_loaded, 16 * j + 16)
                pool.sem_inc(passed["pool"], 1)
                nc.gpsimd.tensor_copy(c_hi[:], c_in[:]).then_inc(c_rounded, 1)
                pool.wait_ge(c_rounded, j + 1)
                nc.gpsimd.tensor_tensor(c_lo[:], c_in[:], c_hi[:].bitcast(F32), ALU.subtract).then_inc(c_split, 1)

            def diagonal_keys(j, l):
                n = NARROW.index(l)
                pool.wait_ge(fill_read, FREE + fills(j, "kn"))
                keys = k_narrow[:, n, :].rearrange("p (b k) -> p b k", b=STREAMS)
                for b in range(STREAMS):
                    last = nc.gpsimd.tensor_tensor(
                        k_diag[:, b], keys[:, b].unsqueeze(1).broadcast_to([P, REP, S]),
                        rep_mask.unsqueeze(2).broadcast_to([P, REP, S]), ALU.mult)
                last.then_inc(k_diag_made, 1)

            def diagonal_rest(j, l):
                pool.wait_ge(kd_hi_made, 2 * j + NARROW.index(l) + 1)
                nc.gpsimd.tensor_tensor(kd_lo[l][:], k_diag[:], kd_hi[l][:].bitcast(F32),
                                        ALU.subtract).then_inc(kd_lo_made, 1)

            def inverse_root(j, l, b):
                pool.wait_ge(rms_out, narrow_uses(j, l, b))
                nc.gpsimd.tensor_tensor(inv_rms[:, b:b + 1], rms[:, b:b + 1], half_power[:],
                                        ALU.pow).then_inc(rms_made, 1)

            def normalise(j, l, b, h, side):
                n = octet(l, b, h)
                pool.wait_ge(inv_made[side], OCTETS * j + n + 1)
                p4 = probs[:, n % 2, side, :].rearrange("p (h k) -> p h k", h=4)
                nc.gpsimd.tensor_tensor(
                    p4, p4, inv[:, n % 2, side, :].unsqueeze(2).broadcast_to([P, 4, S]), ALU.mult,
                ).then_inc(probs_made[side], 1)

            def turn(i, last):
                for slot, phase, fb, front_at, bb, back_at, _ in slot_work(i, last):
                    j, l = back_at
                    wide_front = front_at and front_at[1] not in NARROW
                    if phase == 0 and not wide_front:
                        normalise(j, l, bb, 1, 0)
                        normalise(j, l, bb, 1, 1)
                        if front_at and front_at[1] in NARROW:
                            inverse_root(*front_at, fb)
                    if phase == 0 and wide_front:
                        normalise(j, l, bb, 1, 0)
                        normalise(j, l, bb, 1, 1)
                    if phase == 2:
                        if front_at:
                            normalise(*front_at, fb, 0, 0)
                            normalise(*front_at, fb, 0, 1)
                    if slot == KEYS3_SLOT:
                        diagonal_keys(i, 3)
                    if slot == KEYS3_SLOT + 3:
                        diagonal_rest(i, 3)
                    if not last and slot == SPLIT_SLOT:
                        pool.wait_ge(fill_full, fills(i, "v2.3"))
                        split_context(i + 1)
                    if not last and slot == KEYS0_SLOT:
                        diagonal_keys(i + 1, 0)
                    if not last and slot == KEYS0_SLOT + 3:
                        diagonal_rest(i + 1, 0)

            split_context(0)
            pool.wait_ge(smalls_loaded, 16)
            diagonal_keys(0, 0)
            inverse_root(0, 0, 0)
            diagonal_rest(0, 0)
            normalise(0, 0, 0, 0, 0)
            normalise(0, 0, 0, 0, 1)
            with pool.Fori(0, TURNS - 1) as i:
                turn(i, False)
            turn(TURNS - 1, True)

        @block.scalar
        def _(act):
            def round_weights(which):
                for n in which:
                    w, cols = loads[n]
                    act.wait_ge(stage_loaded[n % STAGES], 16 * (n // STAGES + 1))
                    nc.scalar.activation(w_hi[:, w, cols], stages[n % STAGES], ACT.Copy).then_inc(stage_hi, 1)

            def fill_out(j, name, banks=1):
                if name == "kn":
                    dst = k_narrow[:].rearrange("p l t -> p (l t)")
                elif name == "vn":
                    act.wait_ge(fill_full, fills(j, name))
                    act.wait_ge(zeros_made, 1)
                    columns = v_narrow[:].rearrange("p b l r (g q d) -> p (b l) r g q d", g=KV_HEADS, q=REP)
                    for r in range(REP):
                        last = nc.scalar.activation(
                            columns[:, :, r, :, r, :],
                            fill_bank(banks, name)[:, 0:2 * STREAMS * KV_C].rearrange("p (n g d) -> p n g d",
                                                                                      n=2 * STREAMS, g=KV_HEADS),
                            ACT.Copy)
                    last.then_inc(fill_read, 1)
                    return
                elif name[0] == "k":
                    l, n = int(name[1]), int(name[3])
                    dst = kT[l][:, 2 * n:2 * n + 2, :].rearrange("p c t -> p (c t)")
                else:
                    l, n = int(name[1]), int(name[3])
                    dst = v[l][:, n // 2, n % 2 * BANK:(n % 2 + 1) * BANK]
                act.wait_ge(fill_full, fills(j, name))
                nc.scalar.activation(dst, fill_bank(banks, name)[:], ACT.Copy).then_inc(fill_read, 1)

            def diagonal_keys(j, l):
                act.wait_ge(k_diag_made, 2 * j + NARROW.index(l) + 1)
                nc.scalar.activation(kd_hi[l][:].rearrange("p b r k -> p (b r k)"),
                                     k_diag[:].rearrange("p b r k -> p (b r k)"), ACT.Copy).then_inc(kd_hi_made, 1)

            def wide_queries(j, l, b, part):
                act.wait_ge(q_full, q_uses(j, l, b, part))
                nc.scalar.activation(qT[:, 4 * part:4 * part + 4, b, :], q_ps[:].rearrange("p (c t) -> p c t", c=4),
                                     ACT.Copy, scale=-WIDE_D ** -0.5).then_inc(q_read, 1)

            def outputs_out(j, l, b, h):
                if l in NARROW:
                    act.wait_ge(o_full[b], o_uses(j, l, "pv"))
                    nc.scalar.activation(oT[:, 0, b, :], o_ps[b][:, 0:T], ACT.Copy).then_inc(o_read[b], 1)
                else:
                    act.wait_ge(o_full[b], o_uses(j, l, f"pv{h}"))
                    nc.scalar.activation(oT[:, 4 * h:4 * h + 4, b, :], o_ps[b][:].rearrange("p (c q) -> p c q", c=4),
                                         ACT.Copy).then_inc(o_read[b], 1)

            def exponentials(j, l, b, h, side):
                n = octet(l, b, h)
                act.wait_ge(scores_read[side], FREE + OCTETS * j + n + 1)
                for q in range(4):
                    e = probs[:, n % 2, side, q * S:(q + 1) * S]
                    last = nc.scalar.activation(e, e, ACT.Exp, scale=-1.0, bias=negmax[:, n % 2, side, q:q + 1],
                                                accum_out=rowsum[:, n % 2, side, q:q + 1])
                last.then_inc(exps_made[side], 1)

            def turn(i, last):
                for slot, phase, fb, front_at, bb, back_at, fill in slot_work(i, last):
                    j, l = back_at
                    wide_front = front_at and front_at[1] not in NARROW
                    if phase == 0 and not wide_front:
                        for at, name in fill:
                            fill_out(at, name)
                        if l not in NARROW:
                            outputs_out(j, l, bb, 0)
                    if phase == 0 and wide_front:
                        wide_queries(*front_at, fb, 0)
                        for at, name in fill:
                            fill_out(at, name)
                        if l not in NARROW:
                            outputs_out(j, l, bb, 0)
                    if phase == 1:
                        if front_at:
                            exponentials(*front_at, fb, 0, 0)
                        for at, name in fill:
                            fill_out(at, name)
                        if front_at:
                            exponentials(*front_at, fb, 0, 1)
                    if phase == 2:
                        if front_at:
                            exponentials(*front_at, fb, 1, 0)
                        for at, name in fill:
                            fill_out(at, name)
                        if front_at:
                            exponentials(*front_at, fb, 1, 1)
                    if slot == KEYS3_SLOT + 2:
                        diagonal_keys(i, 3)
                    if not last and slot == KEYS0_SLOT + 2:
                        diagonal_keys(i + 1, 0)

            round_weights(K1_LOADS[:1])
            fill_out(0, "kn")
            round_weights(K1_LOADS[1:])
            diagonal_keys(0, 0)
            round_weights(V1_LOADS)
            fill_out(0, "k1.0", banks=2)
            round_weights(WIDE2_LOADS[0:2])
            for name in ("k1.1", "k1.2"):
                fill_out(0, name, banks=2)
            round_weights(WIDE2_LOADS[2:3])
            fill_out(0, "k1.3", banks=2)
            exponentials(0, 0, 0, 0, 0)
            round_weights(WIDE2_LOADS[3:4])
            exponentials(0, 0, 0, 0, 1)
            for name in ("v1.0", "v1.1", "v1.2"):
                fill_out(0, name, banks=2)
            exponentials(0, 0, 0, 1, 0)
            for name in ("v1.3", "vn"):
                fill_out(0, name, banks=2)
            exponentials(0, 0, 0, 1, 1)
            act.wait_ge(stage_lo, len(loads))
            with act.Fori(0, TURNS - 1) as i:
                turn(i, False)
            turn(TURNS - 1, True)

        @block.vector
        def _(dve):
            steps = [0]

            def setup(ins):
                steps[0] += 1
                ins.then_inc(setup_step, 1)
                dve.wait_ge(setup_step, steps[0])

            def norm_weights():
                for n in range(2):
                    wq = wn[:, NQ + n * C:NQ + (n + 1) * C]
                    nc.vector.tensor_scalar(wq, wq, vec[:, n:n + 1], None, ALU.mult).then_inc(norms_folded, 1)

            def match_tokens():
                setup(nc.vector.tensor_copy(key_f[:], key_i[:]))
                setup(nc.vector.tensor_copy(tok_f[:, :, 0:2], tok_i[:]))
                setup(nc.vector.tensor_scalar(tok_f[:, :, 2:4], tok_f[:, :, 0:2], float(S), None, ALU.add))
                shape = [P, LAYER_MASKS, S, 4]
                setup(nc.vector.tensor_tensor(equal, key_f[:].unsqueeze(1).unsqueeze(3).broadcast_to(shape),
                                              tok_f[:].unsqueeze(2).broadcast_to(shape), ALU.is_equal))

            def column_bias():
                setup(nc.vector.tensor_reduce(hits[:], equal, mybir.AxisListType.X, ALU.max))
                of_mask = hits[:].rearrange("p (l m) s -> p m l s", m=2)
                setup(nc.vector.tensor_scalar(suppress[:], mask, -SUPPRESS, SUPPRESS, ALU.mult, ALU.add))
                setup(nc.vector.tensor_scalar(free[:], of_mask[:, 1], -1.0, 1.0, ALU.mult, ALU.add))
                setup(nc.vector.tensor_tensor(free[:], free[:], of_mask[:, 0], ALU.mult))
                setup(nc.vector.tensor_scalar(col_bias[:, 0:2, :], of_mask[:, 1], suppress[:, 1:2], None, ALU.mult))
                setup(nc.vector.scalar_tensor_tensor(
                    out=col_bias[:, 0:2, :], in0=free[:], scalar=suppress[:, 0:1], in1=col_bias[:, 0:2, :],
                    op0=ALU.mult, op1=ALU.add))

            def split_weights(which):
                for n in which:
                    w, cols = loads[n]
                    dve.wait_ge(stage_hi, n + 1)
                    nc.vector.tensor_tensor(w_lo[:, w, cols], stages[n % STAGES], w_hi[:, w, cols].bitcast(F32),
                                            ALU.subtract).then_inc(stage_lo, 1)

            def square(b, src):
                nc.vector.tensor_tensor(x_sq[:, b, :], src, src, ALU.mult).then_inc(sq_ready, 1)

            def narrow_queries(j, l, b):
                use = narrow_uses(j, l, b)
                dve.wait_ge(q_full, q_uses(j, l, b, 0))
                nc.vector.tensor_scalar(rms[:, b:b + 1], q_ps[:, T:T + 1], EPS, None, ALU.add).then_inc(rms_out, 1)
                nc.vector.tensor_tensor(
                    q_group[:], q_ps[:, 0:T].unsqueeze(1).broadcast_to([P, KV_HEADS, T]),
                    group_mask.unsqueeze(2).broadcast_to([P, KV_HEADS, T]), ALU.mult).then_inc(qg_made, 1)
                dve.wait_ge(qg_made, use)
                dve.sem_inc(q_read, 1)
                nc.vector.tensor_copy(qg_hi[:], q_group[:]).then_inc(qg_hi_made, 1)
                dve.wait_ge(qg_hi_made, use)
                nc.vector.tensor_tensor(qg_lo[:], q_group[:], qg_hi[:].bitcast(F32),
                                        ALU.subtract).then_inc(qg_lo_made, 1)

            def wide_queries(j, l, b, part):
                dve.wait_ge(q_full, q_uses(j, l, b, part))
                nc.vector.tensor_scalar(qT[:, 4 * part:4 * part + 4, b, :],
                                        q_ps[:].rearrange("p (c t) -> p c t", c=4), -WIDE_D ** -0.5, None,
                                        ALU.mult).then_inc(q_read, 1)

            def scores_out(j, l, b, h, side):
                n = octet(l, b, h)
                bias = col_bias[:, 2 if l in NARROW else l - 1, :]
                scale = inv_rms[:, b:b + 1] if l in NARROW else 1.0
                if l in NARROW and h == 0 and side == 0:
                    dve.wait_ge(rms_made, narrow_uses(j, l, b))
                    dve.sem_inc(passed["dve"], 1)
                dve.wait_ge(scores_full[side], OCTETS * j + n + 1)
                dve.sem_inc(passed["dve"], 1)
                for q in range(4):
                    cols = slice(q * S, (q + 1) * S)
                    last = nc.vector.tensor_tensor_reduce(
                        out=probs[:, n % 2, side, cols], in0=scores_ps[side][:, cols], in1=bias, scale=scale,
                        scalar=HUGE, op0=ALU.add, op1=ALU.min, accum_out=negmax[:, n % 2, side, q:q + 1])
                last.then_inc(scores_read[side], 1)

            def inverse_sums(j, l, b, h, side):
                n = octet(l, b, h)
                dve.wait_ge(exps_made[side], OCTETS * j + n + 1)
                nc.vector.reciprocal(inv[:, n % 2, side, :], rowsum[:, n % 2, side, :]).then_inc(inv_made[side], 1)

            def transposes_out(j, l, b, h, side):
                n = octet(l, b, h)
                dve.wait_ge(pt_full[side], OCTETS * j + n + 1)
                nc.vector.tensor_copy(probsT[:, side, :], pt_ps[side][:]).then_inc(pt_read[side], 1)

            def outputs_out(j, l, b, h):
                if l in NARROW:
                    dve.wait_ge(o_full[b], o_uses(j, l, "pv"))
                    nc.vector.tensor_copy(oT[:, 0, b, :], o_ps[b][:, 0:T]).then_inc(o_read[b], 1)
                else:
                    dve.wait_ge(o_full[b], o_uses(j, l, f"pv{h}"))
                    nc.vector.tensor_copy(oT[:, 4 * h:4 * h + 4, b, :],
                                          o_ps[b][:].rearrange("p (c q) -> p c q", c=4)).then_inc(o_read[b], 1)

            def add_input(j, l, b):
                if l == 3:
                    dve.wait_ge(out_stored[b], 16 * j + 16)
                    dve.sem_inc(passed["dve"], 1)
                dve.wait_ge(o_full[b], o_uses(j, l, "o"))
                y = o_ps[b][:, 0:T]
                if l == 0:
                    ins = nc.vector.tensor_tensor(x[:, b, :], y, x_in[:, b, :], ALU.add)
                elif l < 3:
                    ins = nc.vector.scalar_tensor_tensor(out=x[:, b, :], in0=y, scalar=vec[:, l + 1:l + 2],
                                                         in1=x[:, b, :], op0=ALU.add, op1=ALU.add)
                else:
                    ins = nc.vector.tensor_tensor(x_out[:, b, :], y, x[:, b, :], ALU.add)
                ins.then_inc(o_read[b], 1)
                if l == 2:
                    dve.wait_ge(o_read[b], FREE + o_uses(j, l, "o"))
                    square(b, x[:, b, :])

            def input_squares(j, l, b):
                if l == 0:
                    dve.wait_ge(x_loaded, 16 * j + 16)
                    square(b, x_in[:, b, :])

            def front_queries(j, l, b, part):
                if l in NARROW and part == 0:
                    narrow_queries(j, l, b)
                if l not in NARROW:
                    wide_queries(j, l, b, part)

            def turn(i, last):
                for slot, phase, fb, front_at, bb, back_at, _ in slot_work(i, last):
                    j, l = back_at
                    wide_front = front_at and front_at[1] not in NARROW
                    if phase == 0 and not wide_front:
                        if front_at:
                            input_squares(*front_at, fb)
                        inverse_sums(j, l, bb, 1, 0)
                        transposes_out(j, l, bb, 0, 0)
                        transposes_out(j, l, bb, 0, 1)
                        inverse_sums(j, l, bb, 1, 1)
                        if front_at:
                            front_queries(*front_at, fb, 0)
                            front_queries(*front_at, fb, 1)
                    if phase == 0 and wide_front:
                        inverse_sums(j, l, bb, 1, 0)
                        transposes_out(j, l, bb, 0, 0)
                        transposes_out(j, l, bb, 0, 1)
                        inverse_sums(j, l, bb, 1, 1)
                        front_queries(*front_at, fb, 1)
                    if phase == 1:
                        transposes_out(j, l, bb, 1, 0)
                        transposes_out(j, l, bb, 1, 1)
                        if front_at:
                            scores_out(*front_at, fb, 0, 0)
                            scores_out(*front_at, fb, 0, 1)
                        outputs_out(j, l, bb, 1)
                    if phase == 2:
                        if front_at:
                            inverse_sums(*front_at, fb, 0, 0)
                            scores_out(*front_at, fb, 1, 0)
                            inverse_sums(*front_at, fb, 0, 1)
                            scores_out(*front_at, fb, 1, 1)
                        add_input(j, l, bb)

            for s in (fill_read, q_read, *scores_read, *pt_read, *o_read):
                dve.sem_inc(s, FREE)
            for s in out_stored:
                dve.sem_inc(s, 16)
            nc.vector.memset(col_bias[:, 2, :], 0.0)
            dve.wait_ge(keys_made, 1)
            dve.wait_ge(tokens_loaded, 16)
            match_tokens()
            input_squares(0, 0, 0)
            dve.wait_ge(smalls_loaded, 16)
            dve.wait_ge(narrow_qk_loaded, 16)
            norm_weights()
            split_weights(K1_LOADS)
            front_queries(0, 0, 0, 0)
            split_weights(V1_LOADS[:1])
            split_weights(V1_LOADS[1:])
            scores_out(0, 0, 0, 0, 0)
            scores_out(0, 0, 0, 0, 1)
            split_weights(WIDE2_LOADS[0:1])
            column_bias()
            inverse_sums(0, 0, 0, 0, 0)
            split_weights(WIDE2_LOADS[1:3])
            inverse_sums(0, 0, 0, 0, 1)
            scores_out(0, 0, 0, 1, 0)
            split_weights(WIDE2_LOADS[3:4])
            scores_out(0, 0, 0, 1, 1)
            with dve.Fori(0, TURNS - 1) as i:
                turn(i, False)
            turn(TURNS - 1, True)

        @block.tensor
        def _(pe):
            def three(out, stationary, moving):
                for n, ((a_hi, a_lo), (b_hi, b_lo)) in enumerate(zip(stationary, moving)):
                    nc.tensor.matmul(out, a_hi, b_hi, start=(n == 0), stop=False)
                    nc.tensor.matmul(out, a_lo, b_hi, start=False, stop=False)
                    last = nc.tensor.matmul(out, a_hi, b_lo, start=False, stop=(n == len(moving) - 1))
                return last

            def both(first, w, cols):
                return w_hi[:, w, first:first + cols], w_lo[:, w, first:first + cols]

            def project_context(j, name, banks=1):
                pe.wait_ge(fill_read, FREE + fills(j, name) - banks)
                fill_ps = fill_bank(banks, name)
                if name == "kn":
                    pe.wait_ge(c_loaded, 16 * j + 16)
                    for n in range(2):
                        for c in range(CC):
                            first = NK + (n * CC + c) * C
                            last = nc.tensor.matmul(fill_ps[:, n * TOK:(n + 1) * TOK], wn[:, first:first + C],
                                                    c_in[:, c, :], start=(c == 0), stop=(c == CC - 1))
                elif name == "vn":
                    for b in range(STREAMS):
                        for c in range(CC):
                            first = NV + c * 2 * KV_C
                            last = nc.tensor.matmul(fill_ps[:, b * 2 * KV_C:(b + 1) * 2 * KV_C],
                                                    c_in[:, c, b * S:(b + 1) * S], wn[:, first:first + 2 * KV_C],
                                                    start=(c == 0), stop=(c == CC - 1))
                else:
                    pe.wait_ge(c_split, j + 1)
                    l, m = int(name[1]), int(name[3])
                    if name[0] == "k":
                        for n in range(2):
                            chunk = 2 * m + n
                            last = three(fill_ps[:, n * TOK:(n + 1) * TOK],
                                         [both(WK + c * INNER + chunk * P, l - 1, P) for c in range(CC)],
                                         [(c_hi[:, c, :], c_lo[:, c, :]) for c in range(CC)])
                    else:
                        b, n = m // 2, m % 2
                        keys = slice(b * S, (b + 1) * S)
                        last = three(fill_ps[:], [(c_hi[:, c, keys], c_lo[:, c, keys]) for c in range(CC)],
                                     [both(WV + c * INNER + n * BANK, l - 1, BANK) for c in range(CC)])
                last.then_inc(fill_full, 1)

            def queries(j, l, b, part):
                if l in NARROW and part == 1:
                    return
                use = q_uses(j, l, b, part)
                pe.wait_ge(q_read, FREE + use - 1)
                if l in NARROW:
                    pe.wait_ge(sq_ready, narrow_uses(j, l, b))
                    first = NQ + NARROW.index(l) * C
                    src = (x_in if l == 0 else x)[:, b, :]
                    nc.tensor.matmul(q_ps[:, 0:T], wn[:, first:first + C], src, start=True, stop=True)
                    nc.tensor.matmul(q_ps[:, T:2 * T], x_sq[:, b, :], mean_w[:], start=True,
                                     stop=True).then_inc(q_full, 1)
                    return
                if part == 0:
                    pe.wait_ge(qo_loaded, 16)
                    pe.wait_ge(o_read[b], FREE + o_uses(j, l - 1, "o"))
                for n in range(4):
                    first = WQ + (4 * part + n) * P
                    last = nc.tensor.matmul(q_ps[:, n * T:(n + 1) * T], w_qo[:, l - 1, first:first + P], x[:, b, :],
                                            start=True, stop=True)
                last.then_inc(q_full, 1)

            def scores(j, l, b, h):
                n = octet(l, b, h)
                pe.wait_ge(scores_read[0], FREE + OCTETS * j + n)
                if l in NARROW:
                    pe.wait_ge(kd_lo_made, 2 * j + NARROW.index(l) + 1)
                    pe.wait_ge(qg_lo_made, narrow_uses(j, l, b))
                    for side in range(2):
                        g = 2 * h + side
                        if side == 1:
                            pe.wait_ge(scores_read[1], FREE + OCTETS * j + n)
                        three(scores_ps[side][:], [(qg_hi[:, g, :], qg_lo[:, g, :])],
                              [(kd_hi[l][:, b].rearrange("p r k -> p (r k)"),
                                kd_lo[l][:, b].rearrange("p r k -> p (r k)"))]).then_inc(scores_full[side], 1)
                    return
                if h == 0:
                    pe.wait_ge(fill_read, FREE + fills(j, f"k{l}.3"))
                pe.wait_ge(q_read, FREE + q_uses(j, l, b, h))
                for side in range(2):
                    rows = slice(side * WIDE_D, (side + 1) * WIDE_D)
                    if side == 1:
                        pe.wait_ge(scores_read[1], FREE + OCTETS * j + n)
                    for c in range(4):
                        last = nc.tensor.matmul(scores_ps[side][:, c * S:(c + 1) * S], qT[rows, 4 * h + c, b, :],
                                                kT[l][rows, 4 * h + c, b * S:(b + 1) * S], start=True, stop=True)
                    last.then_inc(scores_full[side], 1)

            def transpose_probs(j, l, b, h):
                n = octet(l, b, h)
                for side in range(2):
                    pe.wait_ge(probs_made[side], OCTETS * j + n + 1)
                    pe.wait_ge(pt_read[side], FREE + OCTETS * j + n)
                    for q in range(4):
                        cols = slice(q * S, (q + 1) * S)
                        last = nc.tensor.transpose(pt_ps[side][:, cols], probs[:, n % 2, side, cols], identity)
                    last.then_inc(pt_full[side], 1)

            def weighted_values(j, l, b, h):
                n = octet(l, b, h)
                if l in NARROW:
                    if h == 0:
                        pe.wait_ge(o_read[b], FREE + o_uses(j, l, "pv") - 1)
                        pe.wait_ge(fill_read, FREE + fills(j, "vn"))
                    for side in range(2):
                        pe.wait_ge(pt_read[side], FREE + OCTETS * j + n + 1)
                    for r in range(REP):
                        for side in range(2):
                            rows = slice(32 * (2 * h + side), 32 * (2 * h + side) + 32)
                            last = nc.tensor.matmul(o_ps[b][rows, 0:T], v_narrow[:, b, NARROW.index(l), r, rows],
                                                    probsT[:, side, r * T:(r + 1) * T], start=(r == 0),
                                                    stop=(r == REP - 1))
                    if h == 1:
                        last.then_inc(o_full[b], 1)
                    return
                pe.wait_ge(o_read[b], FREE + o_uses(j, l, f"pv{h}") - 1)
                if h == 0:
                    pe.wait_ge(fill_read, FREE + fills(j, f"v{l}.3"))
                for side in range(2):
                    pe.wait_ge(pt_read[side], FREE + OCTETS * j + n + 1)
                for c in range(4):
                    for side in range(2):
                        head = 8 * h + 2 * c + side
                        last = nc.tensor.matmul(
                            o_ps[b][side * WIDE_D:(side + 1) * WIDE_D, c * T:(c + 1) * T],
                            v[l][:, b, head * WIDE_D:(head + 1) * WIDE_D], probsT[:, side, c * T:(c + 1) * T],
                            start=True, stop=True)
                last.then_inc(o_full[b], 1)

            def output_projection(j, l, b):
                pe.wait_ge(o_read[b], FREE + o_uses(j, l, "o") - 1)
                for c in range(1 if l in NARROW else IC):
                    if l in NARROW:
                        first = NO + NARROW.index(l) * C
                        w = wn[:, first:first + C]
                    else:
                        first = WO + c * C
                        w = w_qo[:, l - 1, first:first + C]
                    last = nc.tensor.matmul(o_ps[b][:, 0:T], w, oT[:, c, b, :], start=(c == 0),
                                            stop=(c == (1 if l in NARROW else IC) - 1))
                last.then_inc(o_full[b], 1)

            def turn(i, last):
                for slot, phase, fb, front_at, bb, back_at, fill in slot_work(i, last):
                    wide_front = front_at and front_at[1] not in NARROW
                    if phase == 0 and not wide_front:
                        transpose_probs(*back_at, bb, 0)
                        if front_at:
                            queries(*front_at, fb, 0)
                            queries(*front_at, fb, 1)
                        for at, name in fill:
                            project_context(at, name)
                        weighted_values(*back_at, bb, 0)
                    if phase == 0 and wide_front:
                        transpose_probs(*back_at, bb, 0)
                        queries(*front_at, fb, 0)
                        weighted_values(*back_at, bb, 0)
                        queries(*front_at, fb, 1)
                        for at, name in fill:
                            project_context(at, name)
                    if phase == 1 and not wide_front:
                        transpose_probs(*back_at, bb, 1)
                        if front_at:
                            scores(*front_at, fb, 0)
                        weighted_values(*back_at, bb, 1)
                        for at, name in fill:
                            project_context(at, name)
                    if phase == 1 and wide_front:
                        transpose_probs(*back_at, bb, 1)
                        scores(*front_at, fb, 0)
                        for at, name in fill:
                            project_context(at, name)
                        weighted_values(*back_at, bb, 1)
                    if phase == 2:
                        if front_at:
                            scores(*front_at, fb, 1)
                        output_projection(*back_at, bb)
                        for at, name in fill:
                            project_context(at, name)

            pe.wait_ge(narrow_qk_loaded, 16)
            project_context(0, "kn")
            pe.wait_ge(norms_folded, 2)
            pe.wait_ge(ones_made, 1)
            queries(0, 0, 0, 0)
            pe.wait_ge(stage_lo, K1_LOADS[-1] + 1)
            for name in ("k1.0", "k1.1"):
                project_context(0, name, banks=2)
            scores(0, 0, 0, 0)
            for name in ("k1.2", "k1.3"):
                project_context(0, name, banks=2)
            pe.wait_ge(stage_lo, V1_LOADS[-1] + 1)
            project_context(0, "v1.0", banks=2)
            scores(0, 0, 0, 1)
            for name in ("v1.1", "v1.2", "v1.3"):
                project_context(0, name, banks=2)
            pe.wait_ge(narrow_vo_loaded, 16)
            project_context(0, "vn", banks=2)
            pe.wait_ge(stage_lo, len(loads))
            pe.wait_ge(smalls_loaded, 16)
            with pe.Fori(0, TURNS - 1) as i:
                turn(i, False)
            turn(TURNS - 1, True)


def kernel(**inputs):
    from concourse import bacc
    from concourse.bass_utils import run_bass_kernel_spmd

    a = {k: np.ascontiguousarray(x) for k, x in inputs.items()}

    def chunks(w):
        return w.reshape(-1, P, w.shape[1]).transpose(1, 0, 2).reshape(P, -1)

    def narrow_keys(w):
        w = np.repeat(w.reshape(CT, KV_HEADS, 1, NARROW_D), REP, axis=2)
        return chunks(w.reshape(CT, P))

    narrow_w = np.concatenate(
        [a[f"L{l}_xattn_wq"] for l in NARROW] + [narrow_keys(a[f"L{l}_xattn_wk"]) for l in NARROW]
        + [chunks(np.concatenate([a[f"L{l}_xattn_wv"] for l in NARROW], axis=1))]
        + [a[f"L{l}_xattn_wo"] for l in NARROW], axis=1)
    kv_w, qo_w = (np.stack([np.concatenate([chunks(a[f"L{l}_xattn_{w}"]) for w in names], axis=1) for l in (1, 2)],
                           axis=1) for names in (("Wk", "Wv"), ("Wq", "Wo")))
    vectors = [a[name] for name in ("L0_xattn_norm_w", "L3_xattn_norm_w", "L1_xattn_bo", "L2_xattn_bo",
                                    "mask_S_fk1", "mask_S_fk0")]
    tokens = np.concatenate([a[f"L{l}_xattn_token_indices_{m}"] for l in (1, 2) for m in "AB"])[None, :]
    if tokens.dtype.itemsize == 8:
        tokens = tokens.view(np.int32)[:, ::2]
    row = np.arange(P)
    constants = np.concatenate([np.eye(P), row[:, None] // NARROW_D % REP == np.arange(REP),
                                (row[:, None] // (NARROW_D * REP) == np.arange(KV_HEADS))
                                * -(1.0 / np.sqrt(np.float32(NARROW_D)))], axis=1)
    arrays = {
        "xT": a["x"].reshape(B * T, C).T,
        "ctxT": a["ctx_2048"].reshape(B * S, CC, P).transpose(2, 1, 0),
        "narrow_w": narrow_w, "kv_w": kv_w, "qo_w": qo_w,
        "small": np.concatenate([constants.astype(np.float32), np.stack(vectors, axis=1)], axis=1), "tokens": tokens,
    }
    nc = bacc.Bacc("TRN2", target_bir_lowering=False, num_devices=1)
    arrays = {f"in_{k}": np.ascontiguousarray(x) for k, x in arrays.items()}
    args = [nc.dram_tensor(k, x.shape, mybir.dt.from_np(x.dtype), kind="ExternalInput").ap()
            for k, x in arrays.items()]
    args.append(nc.dram_tensor("outT", (C, B * T), F32, kind="ExternalOutput").ap())
    build(nc, *args)
    r = run_bass_kernel_spmd(nc, [arrays], core_ids=[0])
    return np.ascontiguousarray(r.results[0]["outT"].T).reshape(B, T, C)
```
